# Optimizing a Trainium2 kernel written in Bass

```python
import numpy as np
import jax
import jax.numpy as jnp

def _softmax(x, axis=-1):
    return jax.nn.softmax(x, axis=axis)

def _gelu(x):
    return jax.nn.gelu(x, approximate=True)

def _silu(x):
    return jax.nn.silu(x)

def _sigmoid(x):
    return jax.nn.sigmoid(x)

def _layernorm(x, axis=-1, eps=1e-05):
    m = jnp.mean(x, axis=axis, keepdims=True)
    v = jnp.var(x, axis=axis, keepdims=True)
    return (x - m) / jnp.sqrt(v + eps)

def _scatter_add(tgt, idx, src, axis=0):
    return tgt.at[idx].add(src)

def _segment_sum(src, seg, n):
    return jax.ops.segment_sum(src, seg, n)
kernel_name = 'mk_gnn_resnorm_d2_gnn_r32_878d0b'

def setup_inputs(seed: int=0):
    np.random.seed(seed)
    _w = jnp.asarray

    def _rec_inputs():
        import jax
        import jax.numpy as jnp
        _gk = jax.random.key(seed)
        x = -0.000202 + 1 * jax.random.normal(jax.random.fold_in(_gk, 1), (3125, 64), jnp.float32)
        _s = jax.random.randint(jax.random.fold_in(_gk, 2), (50000,), 0, 3125, jnp.int32)
        _d = jax.random.randint(jax.random.fold_in(_gk, 3), (50000,), 0, 3125, jnp.int32)
        _loop = jnp.arange(3125, dtype=jnp.int32)
        src = jnp.concatenate([_s, _d, _loop])
        dst = jnp.concatenate([_d, _s, _loop])
        _o = jnp.argsort(dst, stable=True)
        src = src[_o]
        dst = dst[_o]
        edge_attr_32 = -8.62073e-06 + 0.999901 * jax.random.normal(jax.random.fold_in(_gk, 12), (103125, 32), jnp.float32)
        return (x, src, dst, edge_attr_32)
    x, src, dst, edge_attr_32 = _rec_inputs()

    def _L0_gnn_setup():
        import jax, jax.numpy as jnp
        import numpy as np
        N_NODES = 3125
        N_EDGES = 31250
        NODE_DIM = 64
        EDGE_DIM = 32
        EPS = 1e-05
        SLOPE = 0.1

        def _mlp2(v, W1, b1, W2, b2):
            h = jax.nn.leaky_relu(v @ W1 + b1, negative_slope=SLOPE)
            return h @ W2 + b2
        key = jax.random.key(seed)
        ks = jax.random.split(key, 8)
        s = 0.05
        return {'x': jax.random.normal(ks[0], (N_NODES, NODE_DIM), dtype=jnp.float32), 'edge_attr': jax.random.normal(ks[1], (N_EDGES, EDGE_DIM), dtype=jnp.float32), 'W1n': jax.random.normal(ks[2], (NODE_DIM, 2 * NODE_DIM), dtype=jnp.float32) * s, 'b1n': jnp.zeros((2 * NODE_DIM,), dtype=jnp.float32), 'W2n': jax.random.normal(ks[3], (2 * NODE_DIM, NODE_DIM), dtype=jnp.float32) * s, 'b2n': jnp.zeros((NODE_DIM,), dtype=jnp.float32), 'W1e': jax.random.normal(ks[4], (EDGE_DIM, NODE_DIM), dtype=jnp.float32) * s, 'b1e': jnp.zeros((NODE_DIM,), dtype=jnp.float32), 'W2e': jax.random.normal(ks[5], (NODE_DIM, NODE_DIM), dtype=jnp.float32) * s, 'b2e': jnp.zeros((NODE_DIM,), dtype=jnp.float32), 'res_w': jnp.ones((1,), dtype=jnp.float32), 'dp_scale': jnp.ones((1,), dtype=jnp.float32), 'gamma': jnp.ones((NODE_DIM,), dtype=jnp.float32), 'beta': jnp.zeros((NODE_DIM,), dtype=jnp.float32), 'edge_index': jax.random.randint(ks[6], (2, N_EDGES), 0, N_NODES, dtype=jnp.int64) if jax.config.jax_enable_x64 else jax.random.randint(ks[6], (2, N_EDGES), 0, N_NODES, dtype=jnp.int32)}
    _L0_gnn_all = _L0_gnn_setup()
    _L0_gnn_in = {k: v for k, v in _L0_gnn_all.items() if k in ('W1n', 'b1n', 'W2n', 'b2n', 'W1e', 'b1e', 'W2e', 'b2e', 'res_w', 'dp_scale', 'gamma', 'beta')}
    del _L0_gnn_all

    def _L1_gnn_setup():
        import jax, jax.numpy as jnp
        import numpy as np
        N_NODES = 3125
        N_EDGES = 1250000
        IN_FEAT = 64
        OUT_FEAT = 64
        key = jax.random.key(seed)
        k_h, k_w, k_b, k_s, k_d = jax.random.split(key, 5)
        h = jax.random.normal(k_h, (N_NODES, IN_FEAT), dtype=jnp.float32)
        W = jax.random.normal(k_w, (OUT_FEAT, 2 * IN_FEAT), dtype=jnp.float32) * 0.05
        b = jax.random.normal(k_b, (OUT_FEAT,), dtype=jnp.float32) * 0.05
        src = jax.random.randint(k_s, (N_EDGES,), 0, N_NODES, dtype=jnp.int64)
        dst = jax.random.randint(k_d, (N_EDGES,), 0, N_NODES, dtype=jnp.int64)
        return {'h': h, 'W': W, 'b': b, 'src': src, 'dst': dst}
    _L1_gnn_all = _L1_gnn_setup()
    _L1_gnn_in = {k: v for k, v in _L1_gnn_all.items() if k in ('W', 'b')}
    del _L1_gnn_all
    return {'x': x, 'src': src, 'dst': dst, 'edge_attr_32': edge_attr_32, 'L0_gnn_W1n': _L0_gnn_in['W1n'], 'L0_gnn_b1n': _L0_gnn_in['b1n'], 'L0_gnn_W2n': _L0_gnn_in['W2n'], 'L0_gnn_b2n': _L0_gnn_in['b2n'], 'L0_gnn_W1e': _L0_gnn_in['W1e'], 'L0_gnn_b1e': _L0_gnn_in['b1e'], 'L0_gnn_W2e': _L0_gnn_in['W2e'], 'L0_gnn_b2e': _L0_gnn_in['b2e'], 'L0_gnn_res_w': _L0_gnn_in['res_w'], 'L0_gnn_dp_scale': _L0_gnn_in['dp_scale'], 'L0_gnn_gamma': _L0_gnn_in['gamma'], 'L0_gnn_beta': _L0_gnn_in['beta'], 'L1_gnn_W': _L1_gnn_in['W'], 'L1_gnn_b': _L1_gnn_in['b']}

def reference(x, src, dst, edge_attr_32, L0_gnn_W1n, L0_gnn_b1n, L0_gnn_W2n, L0_gnn_b2n, L0_gnn_W1e, L0_gnn_b1e, L0_gnn_W2e, L0_gnn_b2e, L0_gnn_res_w, L0_gnn_dp_scale, L0_gnn_gamma, L0_gnn_beta, L1_gnn_W, L1_gnn_b):
    import jax
    import jax.numpy as jnp

    def _L0_gnn_ref(x, edge_attr, W1n, b1n, W2n, b2n, W1e, b1e, W2e, b2e, res_w, dp_scale, gamma, beta, edge_index):
        import jax, jax.numpy as jnp
        import numpy as np
        N_NODES = 3125
        N_EDGES = 31250
        NODE_DIM = 64
        EDGE_DIM = 32
        EPS = 1e-05
        SLOPE = 0.1

        def _mlp2(v, W1, b1, W2, b2):
            h = jax.nn.leaky_relu(v @ W1 + b1, negative_slope=SLOPE)
            return h @ W2 + b2
        num_nodes = x.shape[0]
        x_t = _mlp2(x, W1n, b1n, W2n, b2n)
        e_t = _mlp2(edge_attr, W1e, b1e, W2e, b2e)
        src, dst = (edge_index[0], edge_index[1])
        msgs = x_t[src] * e_t * dp_scale
        aggregated = jax.ops.segment_sum(msgs, dst, num_segments=num_nodes)
        out = x + aggregated * res_w
        mu = jnp.mean(out, axis=-1, keepdims=True)
        var = jnp.mean(jnp.square(out - mu), axis=-1, keepdims=True)
        return (out - mu) * jax.lax.rsqrt(var + EPS) * gamma + beta

    def _L1_gnn_ref(h, W, b, src, dst):
        import jax, jax.numpy as jnp
        import numpy as np
        N_NODES = 3125
        N_EDGES = 1250000
        IN_FEAT = 64
        OUT_FEAT = 64
        n = h.shape[0]
        msum = jax.ops.segment_sum(h[src], dst, num_segments=n)
        deg = jax.ops.segment_sum(jnp.ones(src.shape, h.dtype), dst, num_segments=n)
        h_N = msum / jnp.maximum(deg, 1.0)[:, None]
        h_total = jnp.concatenate([h, h_N], axis=1)
        return h_total @ W.T + b
    edge_index = jnp.stack([src, dst])
    x = _layernorm(x + _L0_gnn_ref(x, edge_attr_32, L0_gnn_W1n, L0_gnn_b1n, L0_gnn_W2n, L0_gnn_b2n, L0_gnn_W1e, L0_gnn_b1e, L0_gnn_W2e, L0_gnn_b2e, L0_gnn_res_w, L0_gnn_dp_scale, L0_gnn_gamma, L0_gnn_beta, edge_index), axis=-1)
    x = _layernorm(x + _L1_gnn_ref(x, L1_gnn_W, L1_gnn_b, src, dst), axis=-1)
    return x

_drawn_inputs = setup_inputs


def setup_inputs(seed=0):
    import zlib

    import numpy as np

    out = dict(_drawn_inputs(seed))
    spreads = {'L0_gnn_b1n': (0.0, 0.1),
     'L0_gnn_b2n': (0.0, 0.1),
     'L0_gnn_b1e': (0.0, 0.1),
     'L0_gnn_b2e': (0.0, 0.1),
     'L0_gnn_gamma': (1.0, 0.2),
     'L0_gnn_beta': (0.0, 0.1)}
    factors = {}
    for name, (base, spread) in spreads.items():
        noise = np.random.default_rng([zlib.crc32(name.encode()), seed]).standard_normal(out[name].shape)
        drawn = base * np.exp(spread * noise) if base else spread * noise
        out[name] = jnp.asarray(drawn.astype(out[name].dtype))
    for name, factor in factors.items():
        out[name] = (out[name] * factor).astype(out[name].dtype)
    return out
```

```python
from contextlib import ExitStack

import concourse.bass as bass
from concourse import mybir

F32 = mybir.dt.float32
I32 = mybir.dt.int32
ALU = mybir.AluOpType
ACT = mybir.ActivationFunctionType
AX_X = mybir.AxisListType.X

P = 128
EPS = 1e-5
SLOPE = 0.1
TILES = 4
GROUP = TILES * P
SLOTS = 2
WINDOW = 448


def up(n, m):
    return -(-n // m)


def gnn_kernel(nc, x_nat, x_t, src_cols, dst_cols, ea_t, W1n, b1n, W2n, b2n, W1e, b1e, W2e, b2e,
               res_w, dp_scale, gamma, beta, W1_t, b1, out):
    N, D = out.shape
    H = W1n.shape[1]
    FE = W1e.shape[0]
    HE = W1e.shape[1]
    BLKS = up(N, P)
    NP = BLKS * P
    GROUPS = src_cols.shape[1] // TILES
    ITERS = GROUPS // SLOTS
    NWIN = up(N, WINDOW)
    MC = D + 1
    QW = up(NP, 7)

    with ExitStack() as ctx:
        def sb(name, shape, dt=F32):
            return ctx.enter_context(nc.sbuf_tensor(name, shape, dt))

        def sem(name):
            return ctx.enter_context(nc.semaphore(name))

        xt_table = nc.dram_tensor("xt_table", [NP, D], F32, kind="Internal")
        x1_table = nc.dram_tensor("x1_table", [NP, D], F32, kind="Internal")

        xT = sb("xT", [D, NP])
        hidT = sb("hidT", [H, NP])
        x_sb = sb("x_sb", [P, BLKS, D])
        xt_sb = sb("xt_sb", [P, BLKS, D])
        x1_sb = sb("x1_sb", [P, BLKS, D])
        sq = sb("sq", [P, BLKS, D])
        stat = sb("stat", [P, 4, BLKS])
        w1n_sb = sb("w1n_sb", [D, H])
        b1n_sb = sb("b1n_sb", [H, 1])
        w2n_sb = sb("w2n_sb", [H, D])
        b2n_bc = sb("b2n_bc", [P, D])
        w1e_bd = sb("w1e_bd", [P, 2, P])
        b1e_sb = sb("b1e_sb", [P, 1])
        b1e_up = sb("b1e_up", [P, 1])
        b1e_lo = sb("b1e_lo", [P, 1])
        b1n_lo = sb("b1n_lo", [H, 1])
        w2e_bd = sb("w2e_bd", [P, P])
        b2e_row = sb("b2e_row", [1, TILES, D])
        ones_row = sb("ones_row", [1, P])
        gam_bc = sb("gam_bc", [P, D])
        bet_bc = sb("bet_bc", [P, D])
        rw_bc = sb("rw_bc", [P, 2])
        scl = sb("scl", [P, 1])
        w1_sb = sb("w1_sb", [P, D])
        b1_bc = sb("b1_bc", [P, D])
        ident = sb("ident", [P, P])
        eps_sb = sb("eps_sb", [P, 1])

        src_sb = sb("src_sb", [P, GROUPS * TILES], I32)
        dst_i = sb("dst_i", [P, GROUPS * TILES], I32)
        dst_sb = sb("dst_sb", [P, GROUPS * TILES])
        iota_w = sb("iota_w", [P, WINDOW])
        idx = sb("idx", [P, SLOTS, TILES], I32)
        dstk = sb("dstk", [P, SLOTS, TILES])
        rel = sb("rel", [P, SLOTS, TILES])
        ea = sb("ea", [P, SLOTS, P])
        hT = sb("hT", [P, SLOTS, 2, 2, P])
        xg = sb("xg", [P, SLOTS, TILES, D])
        msg = sb("msg", [P, SLOTS, TILES, MC])
        oh = sb("oh", [P, SLOTS, TILES, WINDOW])
        aggT = sb("aggT", [MC, max(NWIN * WINDOW, NP)])
        cat = sb("cat", [P, BLKS, 2 * D])
        catT = sb("catT", [P, 2, P])

        ps = ctx.enter_context(nc.psum_tensor("ps", [P, 8, 512], F32))
        ps_h = [ps[:, j, 0:2 * P] for j in range(SLOTS)]
        ps_e = [ps[:, 2 + j, 0:TILES * D] for j in range(SLOTS)]
        ps_w = [ps[0:MC, 4 + j, 0:WINDOW] for j in range(2)]
        ps_t = [ps[:, 6 + j, :] for j in range(2)]

        consts = sem("consts")
        idents = sem("idents")
        zeroed = sem("zeroed")
        loaded = sem("loaded")
        edges_loaded = sem("edges_loaded")
        ones_set = sem("ones_set")
        node_h = sem("node_h")
        node_act = sem("node_act")
        node_mm = sem("node_mm")
        node_sum = sem("node_sum")
        table_written = sem("table_written")
        dst_ready = sem("dst_ready")
        idx_ready = sem("idx_ready")
        slot_turns = sem("slot_turns")
        dstk_ready = sem("dstk_ready")
        ea_landed = [sem(f"ea_landed{j}") for j in range(SLOTS)]
        gathered = [sem(f"gathered{j}") for j in range(SLOTS)]
        h_done = sem("h_done")
        prelu_done = sem("prelu_done")
        et_done = sem("et_done")
        msgs_done = sem("msgs_done")
        rel_done = sem("rel_done")
        oh_done = sem("oh_done")
        win_done = sem("win_done")
        win_added = sem("win_added")
        chain = sem("chain")
        node_lo = sem("node_lo")
        bias_ready = sem("bias_ready")
        trans = sem("trans")
        trans_used = sem("trans_used")
        x1_ready = sem("x1_ready")
        x1_written = sem("x1_written")
        catT_ready = sem("catT_ready")
        lin_done = sem("lin_done")
        root = sem("root")
        stat_ready = sem("stat_ready")
        out_ready = sem("out_ready")
        out_written = sem("out_written")

        block = ctx.enter_context(nc.Block())

        LOADS = 13

        @block.sync
        def _(sp):
            sp.dma_start(xT[:, :], x_t).then_inc(loaded, 16)
            sp.dma_start(w1n_sb[:, :], W1n).then_inc(loaded, 16)
            sp.dma_start(b1n_sb[:, :], b1n.rearrange("(h a) -> h a", a=1)).then_inc(loaded, 16)
            sp.dma_start(w2n_sb[:, :], W2n).then_inc(loaded, 16)
            sp.dma_start(b2n_bc[:, :], b2n.rearrange("(a d) -> a d", a=1).to_broadcast([P, D])).then_inc(loaded, 16)
            sp.dma_start(b1_bc[:, :], b1.rearrange("(a d) -> a d", a=1).to_broadcast([P, D])).then_inc(loaded, 16)
            sp.dma_start(gam_bc[:, :], gamma.rearrange("(a d) -> a d", a=1).to_broadcast([P, D])).then_inc(loaded, 16)
            sp.dma_start(bet_bc[:, :], beta.rearrange("(a d) -> a d", a=1).to_broadcast([P, D])).then_inc(loaded, 16)
            sp.dma_start(rw_bc[:, 0:1], res_w.rearrange("(a d) -> a d", a=1).to_broadcast([P, 1])).then_inc(loaded, 16)
            sp.dma_start(rw_bc[:, 1:2], dp_scale.rearrange("(a d) -> a d", a=1).to_broadcast([P, 1])).then_inc(loaded, 16)
            sp.dma_start(x_sb[:, :, :], x_nat.rearrange("(b p) d -> p b d", p=P)).then_inc(loaded, 16)
            sp.dma_start(w1_sb[:, :], W1_t).then_inc(loaded, 16)
            sp.dma_start(src_sb[:, :], src_cols).then_inc(edges_loaded, 16)
            sp.dma_start(dst_i[:, :], dst_cols).then_inc(edges_loaded, 16)
            sp.wait_ge(zeroed, 1)
            for q in range(4):
                sp.dma_start(w1e_bd[q * FE:(q + 1) * FE, q // 2, (q % 2) * HE:(q % 2 + 1) * HE], W1e).then_inc(consts, 16)
            for q in range(2):
                sp.dma_start(w2e_bd[q * HE:(q + 1) * HE, q * D:(q + 1) * D], W2e).then_inc(consts, 16)
                sp.dma_start(b1e_sb[q * HE:(q + 1) * HE, :], b1e.rearrange("(h a) -> h a", a=1)).then_inc(consts, 16)
            for k in range(TILES):
                sp.dma_start(b2e_row[:, k, :], b2e.rearrange("(a d) -> a d", a=1)).then_inc(consts, 16)
            for j in range(SLOTS):
                sp.dma_start(ea[:, j, :], ea_t[:, j * P:(j + 1) * P]).then_inc(ea_landed[j], 16)
            with sp.Fori(1, ITERS) as i:
                for j in range(SLOTS):
                    sp.wait_ge(h_done, SLOTS * i + j - 1)
                    sp.dma_start(ea[:, j, :], ea_t[:, bass.ds((SLOTS * i + j) * P, P)]).then_inc(ea_landed[j], 16)
            sp.wait_ge(out_ready, 1)
            full = (N // P) * P
            sp.dma_start(out[0:full, :].rearrange("(b p) d -> p b d", p=P), x1_sb[:, 0:N // P, :]).then_inc(out_written, 16)
            sp.dma_start(out[full:N, :], x1_sb[0:N - full, N // P, :]).then_inc(out_written, 16)
            sp.wait_ge(out_written, 32)

        def gather_group(pool, table, j, done, it, first):
            pool.wait_ge(idx_ready, done + SLOTS * it + j + 1)
            if not first:
                pool.wait_ge(msgs_done, done + SLOTS * it + j - 1)
            pool.sem_inc(slot_turns, 1)
            for k in range(TILES):
                nc.gpsimd.indirect_dma_start(
                    out=xg[:, j, k, :], out_offset=None, in_=table[:, :],
                    in_offset=bass.IndirectOffsetOnAxis(ap=idx[:, j, k:k + 1], axis=0)).then_inc(gathered[j], 16)

        @block.gpsimd
        def _(pool):
            nc.gpsimd.iota(iota_w[:, :], pattern=[[1, WINDOW]], base=0, channel_multiplier=0,
                           allow_small_or_imprecise_dtypes=True).then_inc(idents, 1)
            nc.gpsimd.memset(ident[:, :], 0.0).then_inc(idents, 1)
            pool.wait_ge(idents, 2)
            nc.gpsimd.affine_select(out=ident[:, :], in_=ident[:, :], compare_op=ALU.not_equal, fill=1.0,
                                    base=0, pattern=[[-1, P]], channel_multiplier=1).then_inc(idents, 1)
            pool.wait_ge(table_written, 16)
            for layer, table in enumerate((xt_table, x1_table)):
                done = layer * GROUPS
                if layer == 1:
                    pool.wait_ge(x1_written, 16)
                for j in range(SLOTS):
                    gather_group(pool, table, j, done, 0, layer == 0)
                with pool.Fori(1, ITERS) as i:
                    for j in range(SLOTS):
                        gather_group(pool, table, j, done, i, False)

        def copy_keys(act, j, done, it, first):
            g = SLOTS * it + j
            if not first:
                act.wait_ge(gathered[j], 16 * TILES * (done // SLOTS + it))
            nc.scalar.copy(idx[:, j, :], src_sb[:, bass.ds(g * TILES, TILES)]).then_inc(idx_ready, 1)
            if not first:
                act.wait_ge(rel_done, NWIN * (done + g - 1))
            nc.scalar.copy(dstk[:, j, :], dst_sb[:, bass.ds(g * TILES, TILES)]).then_inc(dstk_ready, 1)

        @block.scalar
        def _(act):
            act.wait_ge(bias_ready, 3)
            for c in range(7):
                act.wait_ge(node_h, c + 1)
                w = min(QW, NP - c * QW)
                nc.scalar.activation(hidT[:, c * QW:c * QW + w], ps[:, c, 0:w], ACT.Identity, bias=b1n_lo[:, 0:1],
                                     scale=SLOPE).then_inc(node_lo, 1)
            act.wait_ge(node_sum, 4)
            act.dma_start(xt_table[:, :].rearrange("(b p) d -> p b d", p=P), xt_sb[:, :, :]).then_inc(table_written, 16)
            act.wait_ge(edges_loaded, 32)
            act.wait_ge(dst_ready, 1)
            act.wait_ge(consts, 16 * (8 + TILES))

            def prelu(j, it, first):
                g = SLOTS * it + j
                act.wait_ge(h_done, g + 1)
                if not first:
                    act.wait_ge(et_done, g - 1)
                z = ps_h[j].rearrange("p (a e) -> p a e", a=2)
                nc.scalar.activation(hT[:, j, 0, :, :], z, ACT.Relu, bias=b1e_up[:, 0:1], scale=1.0 - SLOPE)
                nc.scalar.activation(hT[:, j, 1, :, :], z, ACT.Identity, bias=b1e_lo[:, 0:1],
                                     scale=SLOPE).then_inc(prelu_done, 1)

            for j in range(SLOTS):
                copy_keys(act, j, 0, 0, True)
                prelu(j, 0, True)
            with act.Fori(1, ITERS) as i:
                for j in range(SLOTS):
                    copy_keys(act, j, 0, i, False)
                    prelu(j, i, False)

            def roots(n):
                act.wait_ge(stat_ready, n)
                nc.scalar.activation(stat[:, 2, :], stat[:, 1, :], ACT.Sqrt, bias=eps_sb[:, 0:1]).then_inc(root, 1)

            roots(1)
            roots(2)
            act.wait_ge(x1_ready, 1)
            act.dma_start(x1_table[:, :].rearrange("(b p) d -> p b d", p=P), x1_sb[:, :, :]).then_inc(x1_written, 16)
            for j in range(SLOTS):
                copy_keys(act, j, GROUPS, 0, False)
            with act.Fori(1, ITERS) as i:
                for j in range(SLOTS):
                    copy_keys(act, j, GROUPS, i, False)
            roots(3)

        def window_products(pe, j, done, it, first):
            pe.wait_ge(msgs_done, done + SLOTS * it + j + 1)
            for w in range(NWIN):
                n = NWIN * (done + SLOTS * it + j) + w
                b = (NWIN * j + w) % 2
                pe.wait_ge(oh_done, n + 1)
                if not (first and NWIN * j + w < 2):
                    pe.wait_ge(win_added, n - 1)
                for k in range(TILES):
                    mm = nc.tensor.matmul(ps_w[b], msg[:, j, k, :], oh[:, b, k, :], start=(k == 0),
                                          stop=(k == TILES - 1))
                mm.then_inc(win_done, 1)

        @block.tensor
        def _(pe):
            pe.wait_ge(loaded, 16 * 12)
            for c in range(7):
                w = min(QW, NP - c * QW)
                nc.tensor.matmul(ps[:, c, 0:w], w1n_sb[:, :], xT[:, c * QW:c * QW + w], start=True,
                                 stop=True).then_inc(node_h, 1)
            pe.wait_ge(node_act, 7)
            for b in range(BLKS):
                mm = nc.tensor.matmul(ps[:, b // 8, (b % 8) * D:(b % 8 + 1) * D], hidT[:, b * P:(b + 1) * P],
                                      w2n_sb[:, :], start=True, stop=True)
            mm.then_inc(node_mm, 1)
            pe.wait_ge(node_sum, 4)
            pe.wait_ge(consts, 16 * (8 + TILES))
            pe.wait_ge(ones_set, 1)

            def edge_mlp(j, it, first):
                g = SLOTS * it + j
                pe.wait_ge(ea_landed[j], 16 * (it + 1))
                if not first:
                    pe.wait_ge(prelu_done, g - 1)
                for a in range(2):
                    mm = nc.tensor.matmul(ps_h[j][:, a * P:(a + 1) * P], w1e_bd[:, a, :], ea[:, j, :], start=True, stop=True)
                mm.then_inc(h_done, 1)
                if not first:
                    pe.wait_ge(msgs_done, g - 1)
                nc.tensor.matmul(ps_e[j], ones_row[:, :], b2e_row[:, :, :].rearrange("a k d -> a (k d)"), start=True, stop=False)
                pe.wait_ge(prelu_done, g + 1)
                for a in range(2):
                    for part in range(2):
                        mm = nc.tensor.matmul(ps_e[j][:, a * P:(a + 1) * P], hT[:, j, part, a, :], w2e_bd[:, :],
                                              start=False, stop=(a == 1 and part == 1))
                mm.then_inc(et_done, 1)

            for j in range(SLOTS):
                edge_mlp(j, 0, True)
                window_products(pe, j, 0, 0, True)
            with pe.Fori(1, ITERS) as i:
                for j in range(SLOTS):
                    edge_mlp(j, i, False)
                    window_products(pe, j, 0, i, False)

            def back(layer):
                n0 = layer * 4
                for q in range(4):
                    if q >= 2 or layer:
                        pe.wait_ge(trans_used, n0 + q - 1)
                    for b in range(7 * q, min(7 * q + 7, BLKS)):
                        mm = nc.tensor.transpose(ps_t[q % 2][:, (b - 7 * q) * MC:(b - 7 * q + 1) * MC],
                                                 aggT[:, b * P:(b + 1) * P], ident[0:MC, 0:MC])
                    mm.then_inc(trans, 1)

            pe.wait_ge(idents, 3)
            pe.wait_ge(win_added, NWIN * GROUPS)
            back(0)
            for j in range(SLOTS):
                window_products(pe, j, GROUPS, 0, False)
            with pe.Fori(1, ITERS) as i:
                for j in range(SLOTS):
                    window_products(pe, j, GROUPS, i, False)
            pe.wait_ge(win_added, 2 * NWIN * GROUPS)
            back(1)
            for b in range(BLKS):
                if b == 0:
                    pe.wait_ge(x1_ready, 2)
                if b >= 2:
                    pe.wait_ge(catT_ready, b - 1)
                nc.tensor.transpose(ps_t[b % 2][:, 0:P], cat[:, b, :], ident[:, :]).then_inc(trans, 1)
                pe.wait_ge(catT_ready, b + 1)
                mm = nc.tensor.matmul(ps[:, b // 8, (b % 8) * D:(b % 8 + 1) * D], catT[:, b % 2, :], w1_sb[:, :], start=True, stop=True)
            mm.then_inc(lin_done, 1)

        @block.vector
        def _(dve):
            links = [0]

            def link(ins):
                links[0] += 1
                ins.then_inc(chain, 1)
                dve.wait_ge(chain, links[0])

            nc.vector.memset(w1e_bd[:, :, :], 0.0)
            nc.vector.memset(w2e_bd[:, :], 0.0)
            nc.vector.memset(ones_row[:, :], 1.0).then_inc(ones_set, 1)
            nc.vector.memset(eps_sb[:, :], EPS)
            nc.vector.memset(aggT[:, :], 0.0)
            link(nc.vector.memset(msg[:, :, :, :], 1.0))
            nc.vector.sem_inc(zeroed, 1)
            dve.wait_ge(edges_loaded, 32)
            nc.vector.tensor_copy(dst_sb[:, :], dst_i[:, :]).then_inc(dst_ready, 1)
            dve.wait_ge(loaded, 16 * 12)
            link(nc.vector.tensor_tensor(scl[:, :], rw_bc[:, 0:1], rw_bc[:, 1:2], ALU.mult))
            dve.wait_ge(consts, 16 * (8 + TILES))
            nc.vector.tensor_scalar(b1n_lo[:, :], b1n_sb[:, :], SLOPE, None, ALU.mult).then_inc(bias_ready, 1)
            nc.vector.tensor_scalar(b1e_lo[:, :], b1e_sb[:, :], SLOPE, None, ALU.mult).then_inc(bias_ready, 1)
            nc.vector.tensor_scalar(b1e_up[:, :], b1e_sb[:, :], 1.0 - SLOPE, None, ALU.mult).then_inc(bias_ready, 1)
            for c in range(7):
                w = min(QW, NP - c * QW)
                h = hidT[:, c * QW:c * QW + w]
                dve.wait_ge(node_lo, c + 1)
                nc.vector.scalar_tensor_tensor(out=h, in0=ps[:, c, 0:w], scalar=b1n_sb[:, 0:1], in1=h, op0=ALU.add,
                                               op1=ALU.max).then_inc(node_act, 1)
            dve.wait_ge(node_mm, 1)
            for q in range(4):
                nb = min(8, BLKS - 8 * q)
                nc.vector.tensor_tensor(xt_sb[:, 8 * q:8 * q + nb, :], ps[:, q, 0:nb * D].rearrange("p (b d) -> p b d", d=D),
                                        b2n_bc[:, :].rearrange("p (a d) -> p a d", a=1).to_broadcast([P, nb, D]),
                                        ALU.add).then_inc(node_sum, 1)
            dve.wait_ge(idents, 3)

            def window_sums(j, done, it, first):
                g = SLOTS * it + j
                dve.wait_ge(dstk_ready, done + g + 1)
                for w in range(NWIN):
                    n = NWIN * (done + g) + w
                    b = (NWIN * j + w) % 2
                    nc.vector.tensor_scalar(rel[:, b, :], dstk[:, j, :], float(-w * WINDOW), None, ALU.add).then_inc(rel_done, 1)
                    dve.wait_ge(rel_done, n + 1)
                    if not (first and NWIN * j + w < 2):
                        dve.wait_ge(win_done, n - 1)
                    for k in range(TILES):
                        ins = nc.vector.tensor_scalar(oh[:, b, k, :], iota_w[:, :], rel[:, b, k:k + 1], None, ALU.is_equal)
                    ins.then_inc(oh_done, 1)
                    dve.wait_ge(win_done, n + 1)
                    seg = aggT[:, w * WINDOW:(w + 1) * WINDOW]
                    if not (first and j == 0):
                        dve.wait_ge(win_added, n - NWIN + 1)
                    nc.vector.tensor_tensor(seg, ps_w[b], seg, ALU.add).then_inc(win_added, 1)

            def messages(j, it):
                g = SLOTS * it + j
                dve.wait_ge(et_done, g + 1)
                dve.wait_ge(gathered[j], 16 * TILES * (it + 1))
                nc.vector.tensor_tensor(msg[:, j, :, 0:D], ps_e[j].rearrange("p (k d) -> p k d", d=D), xg[:, j, :, :],
                                        ALU.mult).then_inc(msgs_done, 1)

            for j in range(SLOTS):
                messages(j, 0)
                window_sums(j, 0, 0, True)
            with dve.Fori(1, ITERS) as i:
                for j in range(SLOTS):
                    dve.wait_ge(win_done, NWIN * (SLOTS * i + j - 1))
                    messages(j, i)
                    window_sums(j, 0, i, False)

            def row(ap):
                return ap.rearrange("p (a d) -> p a d", a=1).to_broadcast([P, BLKS, D])

            def col(k):
                return stat[:, k, :].rearrange("p (b a) -> p b a", a=1).to_broadcast([P, BLKS, D])

            def layernorm(y, n):
                link(nc.vector.tensor_reduce(stat[:, 0, :], y, AX_X, ALU.add))
                link(nc.vector.tensor_scalar(stat[:, 0, :], stat[:, 0, :], 1.0 / D, None, ALU.mult))
                link(nc.vector.tensor_tensor(y, y, col(0), ALU.subtract))
                link(nc.vector.tensor_tensor(sq[:, :, :], y, y, ALU.mult))
                link(nc.vector.tensor_reduce(stat[:, 1, :], sq[:, :, :], AX_X, ALU.add))
                nc.vector.tensor_scalar(stat[:, 1, :], stat[:, 1, :], 1.0 / D, None, ALU.mult).then_inc(stat_ready, 1)
                dve.wait_ge(root, n)
                link(nc.vector.reciprocal(stat[:, 3, :], stat[:, 2, :]))
                link(nc.vector.tensor_tensor(y, y, col(3), ALU.mult))

            y = x1_sb[:, :, :]
            deg = stat[:, 0, :]
            for q in range(4):
                nb = min(7, BLKS - 7 * q)
                dve.wait_ge(trans, q + 1)
                link(nc.vector.scalar_tensor_tensor(
                    out=x1_sb[:, 7 * q:7 * q + nb, :],
                    in0=ps_t[q % 2][:, 0:nb * MC].rearrange("p (b c) -> p b c", c=MC)[:, :, 0:D],
                    scalar=scl[:, 0:1], in1=x_sb[:, 7 * q:7 * q + nb, :], op0=ALU.mult, op1=ALU.add))
                nc.vector.sem_inc(trans_used, 1)
            layernorm(y, 1)
            link(nc.vector.tensor_tensor(y, y, row(gam_bc[:, :]), ALU.mult))
            link(nc.vector.tensor_tensor(y, y, row(bet_bc[:, :]), ALU.add))
            link(nc.vector.tensor_tensor(y, y, x_sb[:, :, :], ALU.add))
            layernorm(y, 2)
            link(nc.vector.memset(aggT[:, :], 0.0))
            nc.vector.sem_inc(x1_ready, 1)

            def passed(j, it):
                g = SLOTS * it + j
                dve.wait_ge(gathered[j], 16 * TILES * (GROUPS // SLOTS + it + 1))
                nc.vector.tensor_copy(msg[:, j, :, 0:D], xg[:, j, :, :]).then_inc(msgs_done, 1)

            for j in range(SLOTS):
                passed(j, 0)
                window_sums(j, GROUPS, 0, False)
            with dve.Fori(1, ITERS) as i:
                for j in range(SLOTS):
                    passed(j, i)
                    window_sums(j, GROUPS, i, False)

            link(nc.vector.tensor_copy(cat[:, :, 0:D], y))
            for q in range(4):
                nb = min(7, BLKS - 7 * q)
                dve.wait_ge(trans, 4 + q + 1)
                v = ps_t[q % 2][:, 0:nb * MC].rearrange("p (b c) -> p b c", c=MC)
                d = stat[:, 0, 7 * q:7 * q + nb].rearrange("p (b a) -> p b a", a=1)
                link(nc.vector.tensor_scalar(d, v[:, :, D:MC], 1.0, None, ALU.max))
                link(nc.vector.reciprocal(d, d))
                link(nc.vector.tensor_tensor(cat[:, 7 * q:7 * q + nb, D:2 * D], v[:, :, 0:D],
                                             d.to_broadcast([P, nb, D]), ALU.mult))
                nc.vector.sem_inc(trans_used, 1)
            nc.vector.sem_inc(x1_ready, 1)
            for b in range(BLKS):
                dve.wait_ge(trans, 8 + b + 1)
                nc.vector.tensor_copy(catT[:, b % 2, :], ps_t[b % 2][:, 0:P]).then_inc(catT_ready, 1)
            dve.wait_ge(lin_done, 1)
            for q in range(4):
                nb = min(8, BLKS - 8 * q)
                link(nc.vector.tensor_tensor(x1_sb[:, 8 * q:8 * q + nb, :], ps[:, q, 0:nb * D].rearrange("p (b d) -> p b d", d=D),
                                             x1_sb[:, 8 * q:8 * q + nb, :], ALU.add))
            link(nc.vector.tensor_tensor(y, y, row(b1_bc[:, :]), ALU.add))
            layernorm(y, 3)
            nc.vector.sem_inc(out_ready, 1)


def kernel(x, src, dst, edge_attr_32, L0_gnn_W1n, L0_gnn_b1n, L0_gnn_W2n, L0_gnn_b2n, L0_gnn_W1e, L0_gnn_b1e,
           L0_gnn_W2e, L0_gnn_b2e, L0_gnn_res_w, L0_gnn_dp_scale, L0_gnn_gamma, L0_gnn_beta, L1_gnn_W, L1_gnn_b):
    import numpy as np
    import concourse.bacc as bacc
    from concourse import mybir as _mybir
    from concourse.bass_utils import run_bass_kernel_spmd

    x, src, dst, edges = (np.asarray(a) for a in (x, src, dst, edge_attr_32))
    N, D = x.shape
    E, FE = edges.shape
    n_pad = up(N, P) * P
    groups = up(up(E, GROUP), SLOTS) * SLOTS
    e_pad = groups * GROUP

    x_pad = np.zeros((n_pad, D), x.dtype)
    x_pad[:N] = x
    src_pad = np.zeros(e_pad, src.dtype)
    src_pad[:E] = src
    dst_pad = np.full(e_pad, 1 << 14, dst.dtype)
    dst_pad[:E] = dst
    ea_pad = np.zeros((e_pad, FE), edges.dtype)
    ea_pad[:E] = edges
    ea_t = np.ascontiguousarray(ea_pad.reshape(groups, TILES, P, FE).transpose(1, 3, 0, 2).reshape(TILES * FE, groups * P))
    arrays = {
        "x_nat": x_pad, "x_t": np.ascontiguousarray(x_pad.T),
        "src_cols": np.ascontiguousarray(src_pad.reshape(-1, P).T),
        "dst_cols": np.ascontiguousarray(dst_pad.reshape(-1, P).T),
        "ea_t": ea_t,
        "W1n": L0_gnn_W1n, "b1n": L0_gnn_b1n, "W2n": L0_gnn_W2n, "b2n": L0_gnn_b2n,
        "W1e": L0_gnn_W1e, "b1e": L0_gnn_b1e, "W2e": L0_gnn_W2e, "b2e": L0_gnn_b2e,
        "res_w": L0_gnn_res_w, "dp_scale": L0_gnn_dp_scale, "gamma": L0_gnn_gamma, "beta": L0_gnn_beta,
        "W1_t": np.ascontiguousarray(np.asarray(L1_gnn_W).T), "b1": L1_gnn_b,
    }
    arrays = {k: np.ascontiguousarray(v) for k, v in arrays.items()}
    nc = bacc.Bacc("TRN2", target_bir_lowering=False, num_devices=1)
    args = [nc.dram_tensor(k, a.shape, _mybir.dt.from_np(a.dtype), kind="ExternalInput").ap() for k, a in arrays.items()]
    args.append(nc.dram_tensor("out", (N, D), F32, kind="ExternalOutput").ap())
    gnn_kernel(nc, *args)
    r = run_bass_kernel_spmd(nc, [arrays], core_ids=[0])
    return r.results[0]["out"]
```

```python
from contextlib import ExitStack

import concourse.bass as bass
from concourse import mybir

F32 = mybir.dt.float32
F16 = mybir.dt.float16
BF16 = mybir.dt.bfloat16
U32 = mybir.dt.uint32
I32 = mybir.dt.int32
ALU = mybir.AluOpType
ACT = mybir.ActivationFunctionType
AX_X = mybir.AxisListType.X

P = 128
EPS = 1e-5
SLOPE = 0.1
TILES = 4
GROUP = TILES * P
SLOTS = 2
SPAN = 20
WINDOW = 448
PAD_DST = 1 << 14
MAX_COUNT = 256
PARTS = 3


def up(n, m):
    return -(-n // m)


def gnn_kernel(nc, x_nat, x_t, src_cols, dst_rows, dst_cols, ea_t, W1n, b1n, W2n, b2n, W1e, b1e, W2e, b2e,
               res_w, dp_scale, gamma, beta, W1_t, b1, out):
    N, D = out.shape
    H = W1n.shape[1]
    FE = W1e.shape[0]
    HE = W1e.shape[1]
    BLKS = up(N, P)
    NP = BLKS * P
    GROUPS = src_cols.shape[1] // TILES
    ITERS = GROUPS // SLOTS
    NWIN = up(N, WINDOW)
    MC = D + 1
    KEYS = BLKS * SPAN
    CH = 7
    QW = up(NP, CH)
    QUART = [(7 * q, min(7, BLKS - 7 * q)) for q in range(4)]
    BATCH = 5
    NBATCH = BLKS // BATCH
    LO, KEY, REL = range(3)
    assert NBATCH * BATCH == BLKS and KEYS <= 512 and NWIN * WINDOW <= NP

    with ExitStack() as ctx:
        def sem(name):
            return ctx.enter_context(nc.semaphore(name))

        def alloc(scope):
            return lambda name, shape, dt=F32: scope.enter_context(nc.sbuf_tensor(name, shape, dt))

        xt_table = nc.dram_tensor("xt_table", [NP, D], F32, kind="Internal")
        hw_table = nc.dram_tensor("hw_table", [NP, D], F32, kind="Internal")
        base_dram = nc.dram_tensor("base_dram", [1, GROUPS], F32, kind="Internal")
        span_dram = nc.dram_tensor("span_dram", [1, GROUPS], F32, kind="Internal")

        sb = alloc(ctx)
        w1e_bd = sb("w1e_bd", [P, 2, P])
        w2e_bd = sb("w2e_bd", [P, P])
        b2e_row = sb("b2e_row", [1, TILES, D])
        ones_row = sb("ones_row", [1, P])
        ones_col = sb("ones_col", [P, 1])
        b1e_sb = sb("b1e_sb", [P, 1])
        b1e_up = sb("b1e_up", [P, 1])
        b1e_lo = sb("b1e_lo", [P, 1])
        b2n_bc = sb("b2n_bc", [P, D])
        gam_bc = sb("gam_bc", [P, D])
        bet_bc = sb("bet_bc", [P, D])
        b1_bc = sb("b1_bc", [P, D])
        rw_bc = sb("rw_bc", [P, 2])
        scl = sb("scl", [P, 1])
        wab = sb("wab", [D, 2, D])
        ident = sb("ident", [P, P])
        eps_sb = sb("eps_sb", [P, 1])
        iota_k = sb("iota_k", [P, 512], F16)
        iota_s = sb("iota_s", [P, SPAN])
        flags = sb("flags", [P, 2], I32)
        zero_col = sb("zero_col", [P, 1])
        aggT = sb("aggT", [MC, NP])

        early = ExitStack()
        eb = alloc(early)
        xT = eb("xT", [D, NP])
        hidT = eb("hidT", [H, NP])
        xt_sb = eb("xt_sb", [P, BLKS, D])
        w1n_sb = eb("w1n_sb", [D, H])
        w2n_sb = eb("w2n_sb", [H, D])
        b1n_sb = eb("b1n_sb", [H, 1])
        b1n_lo = eb("b1n_lo", [H, 1])
        dst_i = eb("dst_i", [P, GROUPS * TILES], I32)
        dst_f = eb("dst_f", [P, GROUPS * TILES])
        rows_i = eb("rows_i", [ITERS, SLOTS, GROUP], I32)
        rows_f = eb("rows_f", [ITERS, SLOTS, GROUP])
        low = eb("low", [ITERS, SLOTS])
        high = eb("high", [ITERS, SLOTS])
        base_bc = eb("base_bc", [P, GROUPS])
        span_bc = eb("span_bc", [P, GROUPS])
        widest = eb("widest", [P, 1])
        hi_i = eb("hi_i", [P, GROUPS * TILES], I32)
        lo_i = eb("lo_i", [P, GROUPS * TILES], I32)

        g_src = eb("g_src", [P, GROUPS * TILES], I32)
        g_dst = eb("g_dst", [P, GROUPS * TILES])
        g_dst_i = eb("g_dst_i", [P, GROUPS * TILES], I32)
        g_iota = eb("g_iota", [P, WINDOW])
        g_key = eb("g_key", [P, SLOTS, TILES])
        g_rel = eb("g_rel", [P, 2, TILES])
        g_oh = eb("g_oh", [P, 2, TILES, WINDOW])
        g_idx = eb("g_idx", [P, SLOTS, TILES], I32)
        g_xg = eb("g_xg", [P, SLOTS, TILES, D])
        g_msg = eb("g_msg", [P, SLOTS, TILES, MC])
        early.close()

        A = sb("A", [P, BLKS, NP], BF16)
        EARLY_BLKS = 9
        assert 4 * (2 * NP + BLKS * D + 4 * GROUPS * TILES + 2 * SLOTS * GROUP + 2 * GROUPS + 4 * D) <= EARLY_BLKS * NP * 2

        loop = ExitStack()
        lb = alloc(loop)
        src_sb = lb("src_sb", [P, GROUPS * TILES], I32)
        keys = lb("keys", [P, GROUPS * 3 * TILES], F16)
        base_i = lb("base_i", [1, GROUPS], I32)
        idx = lb("idx", [P, SLOTS, TILES], I32)
        keyf = lb("keyf", [P, SLOTS, 3 * TILES])
        ea = lb("ea", [P, SLOTS, P])
        hT = lb("hT", [P, SLOTS, 2, 2, P])
        xg = lb("xg", [P, SLOTS, TILES, D])
        msg = lb("msg", [P, SLOTS, TILES, MC])
        oh_lo = lb("oh_lo", [P, SLOTS, TILES, P], BF16)
        oh_key = lb("oh_key", [P, SLOTS, TILES, KEYS], BF16)
        oh_rel = lb("oh_rel", [P, SLOTS, TILES, SPAN])
        loop.close()

        tb = alloc(ctx)
        x_sb = tb("x_sb", [P, BLKS, D])
        x1_sb = tb("x1_sb", [P, BLKS, D])
        parts = tb("parts", [P, BLKS, PARTS, D], BF16)
        sq = tb("sq", [P, 7 * D])
        res = tb("res", [P, 7 * D])
        x1T = tb("x1T", [D, 7, P])
        stat = tb("stat", [P, 4, 7])
        rdeg = tb("rdeg", [P, BLKS])
        heavy = tb("heavy", [P, BLKS])
        n_heavy = tb("n_heavy", [1, 1])

        ps = ctx.enter_context(nc.psum_tensor("ps", [P, 8, 512], F32))
        ps_h = [ps[:, j, 0:2 * P] for j in range(SLOTS)]
        ps_e = [ps[:, 2 + j, 0:TILES * D] for j in range(SLOTS)]
        ps_a = [ps[:, 4 + j, 0:KEYS] for j in range(SLOTS)]
        ps_s = [ps[0:MC, 6 + j, 0:SPAN] for j in range(SLOTS)]
        ps_w = [ps[0:MC, 4 + j, 0:WINDOW] for j in range(2)]
        ps_t = [ps[:, 6 + j, :] for j in range(2)]

        zeroed = sem("zeroed")
        consts = sem("consts")
        loaded = sem("loaded")
        rest_loaded = sem("rest_loaded")
        src_loaded = sem("src_loaded")
        dst_loaded = sem("dst_loaded")
        rows_loaded = sem("rows_loaded")
        iotas = sem("iotas")
        idents = sem("idents")
        bias_ready = sem("bias_ready")
        node_h = sem("node_h")
        node_lo = sem("node_lo")
        node_act = sem("node_act")
        node_mm = sem("node_mm")
        node_sum = sem("node_sum")
        table_written = sem("table_written")
        span_found = sem("span_found")
        span_written = sem("span_written")
        span_back = sem("span_back")
        keys_made = sem("keys_made")
        flag_made = sem("flag_made")
        a_zero = sem("a_zero")
        slot_turns = sem("slot_turns")
        idx_ready = sem("idx_ready")
        keyf_ready = sem("keyf_ready")
        ea_landed = [sem(f"ea_landed{j}") for j in range(SLOTS)]
        gathered = [sem(f"gathered{j}") for j in range(SLOTS)]
        h_done = sem("h_done")
        leaky_done = sem("leaky_done")
        et_done = sem("et_done")
        msgs_done = sem("msgs_done")
        oh_done = sem("oh_done")
        a_done = sem("a_done")
        a_added = sem("a_added")
        s_done = sem("s_done")
        s_added = sem("s_added")
        sums_done = sem("sums_done")
        g_loaded = [sem(f"g_loaded{l}") for l in range(2)]
        g_ready = [sem(f"g_ready{l}") for l in range(2)]
        g_key_ready = [sem(f"g_key_ready{l}") for l in range(2)]
        g_rel_done = [sem(f"g_rel_done{l}") for l in range(2)]
        g_oh_done = [sem(f"g_oh_done{l}") for l in range(2)]
        g_win_done = [sem(f"g_win_done{l}") for l in range(2)]
        g_added = [sem(f"g_added{l}") for l in range(2)]
        g_table = sem("g_table")
        g_table_written = sem("g_table_written")
        g_gathered = [sem(f"g_gathered{j}") for j in range(SLOTS)]
        g_idx_ready = sem("g_idx_ready")
        g_msgs = sem("g_msgs")
        g_back = sem("g_back")
        g_back_used = sem("g_back_used")
        chain = sem("chain")
        x_back = sem("x_back")
        back_done = sem("back_done")
        back_used = sem("back_used")
        stat_ready = sem("stat_ready")
        root = sem("root")
        x1_ready = sem("x1_ready")
        x1t_done = sem("x1t_done")
        x1t_copied = sem("x1t_copied")
        lin_done = sem("lin_done")
        lin_used = sem("lin_used")
        part_hi = sem("part_hi")
        part_res = sem("part_res")
        part_mid = sem("part_mid")
        parts_ready = sem("parts_ready")
        heavy_found = sem("heavy_found")
        heavy_counted = sem("heavy_counted")
        near_done = sem("near_done")
        near_used = sem("near_used")
        out_ready = sem("out_ready")
        out_written = sem("out_written")

        block = ctx.enter_context(nc.Block())

        ACT_BLKS, POOL_BLKS = EARLY_BLKS // 2, BLKS - (BLKS - EARLY_BLKS) // 2

        def a_words(b0, b1):
            return A[:, b0:b1, :].rearrange("p b n -> p (b n)").bitcast(U32)

        CONSTS = 16 * (8 + TILES)
        LOADED = 16 * 5
        REST = 16 * 7

        def row_of(v, n):
            return v.rearrange("(a d) -> a d", a=1).to_broadcast([P, n])

        def natural(table):
            return table[:, :].rearrange("(b p) d -> p b d", p=P)

        def blocks_of(t, nb):
            return t[:, 0:nb * D].rearrange("p (b d) -> p b d", d=D)

        def lin_of(nb):
            return ps[:, 4:6, :].rearrange("p a n -> p (a n)")[:, 0:nb * 2 * D].rearrange("p (b h d) -> p b h d", h=2, d=D)

        def x1t_of(nb):
            return ps[0:D, 2:4, :].rearrange("p a n -> p (a n)")[:, 0:nb * P].rearrange("p (b n) -> p b n", n=P)

        def back_of(q, nb):
            return ps_t[q % 2][:, 0:nb * MC].rearrange("p (b c) -> p b c", c=MC)

        @block.sync
        def _(sp):
            sp.dma_start(xT[:, :], x_t).then_inc(loaded, 16)
            sp.dma_start(w1n_sb[:, :], W1n).then_inc(loaded, 16)
            sp.dma_start(b1n_sb[:, :], b1n.rearrange("(h a) -> h a", a=1)).then_inc(loaded, 16)
            sp.dma_start(w2n_sb[:, :], W2n).then_inc(loaded, 16)
            sp.dma_start(b2n_bc[:, :], row_of(b2n, D)).then_inc(loaded, 16)
            sp.wait_ge(zeroed, 1)
            for q in range(4):
                sp.dma_start(w1e_bd[q * FE:(q + 1) * FE, q // 2, (q % 2) * HE:(q % 2 + 1) * HE], W1e).then_inc(consts, 16)
            for q in range(2):
                sp.dma_start(w2e_bd[q * HE:(q + 1) * HE, q * D:(q + 1) * D], W2e).then_inc(consts, 16)
                sp.dma_start(b1e_sb[q * HE:(q + 1) * HE, :], b1e.rearrange("(h a) -> h a", a=1)).then_inc(consts, 16)
            for k in range(TILES):
                sp.dma_start(b2e_row[:, k, :], b2e.rearrange("(a d) -> a d", a=1)).then_inc(consts, 16)
            for j in range(SLOTS):
                sp.dma_start(ea[:, j, :], ea_t[:, j * P:(j + 1) * P]).then_inc(ea_landed[j], 16)
            sp.dma_start(gam_bc[:, :], row_of(gamma, D)).then_inc(rest_loaded, 16)
            sp.dma_start(bet_bc[:, :], row_of(beta, D)).then_inc(rest_loaded, 16)
            sp.dma_start(b1_bc[:, :], row_of(b1, D)).then_inc(rest_loaded, 16)
            sp.dma_start(rw_bc[:, 0:1], row_of(res_w, 1)).then_inc(rest_loaded, 16)
            sp.dma_start(rw_bc[:, 1:2], row_of(dp_scale, 1)).then_inc(rest_loaded, 16)
            for half in range(2):
                sp.dma_start(wab[:, half, :], W1_t[half * D:(half + 1) * D, :]).then_inc(rest_loaded, 16)
            with sp.Fori(1, ITERS) as i:
                for j in range(SLOTS):
                    sp.wait_ge(h_done, SLOTS * i + j - 1)
                    sp.dma_start(ea[:, j, :], ea_t[:, bass.ds((SLOTS * i + j) * P, P)]).then_inc(ea_landed[j], 16)
            sp.wait_ge(sums_done, 1)
            sp.dma_start(x_sb[:, :, :], x_nat.rearrange("(b p) d -> p b d", p=P)).then_inc(x_back, 16)
            for n in range(NBATCH):
                sp.wait_ge(out_ready, n + 1)
                whole = min(BATCH, N // P - n * BATCH)
                b0 = n * BATCH
                sp.dma_start(out[b0 * P:(b0 + whole) * P, :].rearrange("(b p) d -> p b d", p=P),
                             x_sb[:, b0:b0 + whole, :]).then_inc(out_written, 16)
            full = (N // P) * P
            sp.dma_start(out[full:N, :], x_sb[0:N - full, N // P, :]).then_inc(out_written, 16)
            sp.wait_ge(out_written, 16 * (NBATCH + 1))

        def gather_group(table, index, rows, landed, j):
            for k in range(TILES):
                nc.gpsimd.indirect_dma_start(
                    out=rows[:, j, k, :], out_offset=None, in_=table[:, :],
                    in_offset=bass.IndirectOffsetOnAxis(ap=index[:, j, k:k + 1], axis=0)).then_inc(landed[j], 16)

        @block.gpsimd
        def _(pool):
            nc.gpsimd.iota(iota_k[:, :], pattern=[[1, 512]], base=0, channel_multiplier=0,
                           allow_small_or_imprecise_dtypes=True).then_inc(iotas, 1)
            nc.gpsimd.iota(iota_s[:, :], pattern=[[1, SPAN]], base=0, channel_multiplier=0,
                           allow_small_or_imprecise_dtypes=True).then_inc(iotas, 1)
            nc.gpsimd.memset(ident[:, :], 0.0).then_inc(idents, 1)
            pool.wait_ge(idents, 1)
            nc.gpsimd.affine_select(out=ident[:, :], in_=ident[:, :], compare_op=ALU.not_equal, fill=1.0,
                                    base=0, pattern=[[-1, P]], channel_multiplier=1).then_inc(idents, 1)
            nc.gpsimd.memset(a_words(POOL_BLKS, BLKS), 0).then_inc(a_zero, 1)
            pool.wait_ge(table_written, 16)
            for j in range(SLOTS):
                pool.wait_ge(idx_ready, j + 1)
                gather_group(xt_table, idx, xg, gathered, j)
            with pool.Fori(1, ITERS) as i:
                for j in range(SLOTS):
                    pool.wait_ge(idx_ready, SLOTS * i + j + 1)
                    pool.wait_ge(msgs_done, SLOTS * i + j - 1)
                    pool.sem_inc(slot_turns, 1)
                    gather_group(xt_table, idx, xg, gathered, j)
            pool.wait_ge(flag_made, 2)
            fast = nc.gpsimd.value_load(flags[0:1, 1:2], min_val=0, max_val=1)
            with pool.If(fast == 0):
                pool.wait_ge(g_table_written, 16)
                for j in range(SLOTS):
                    pool.wait_ge(g_idx_ready, j + 1)
                    gather_group(hw_table, g_idx, g_xg, g_gathered, j)
                with pool.Fori(1, ITERS) as i:
                    for j in range(SLOTS):
                        pool.wait_ge(g_idx_ready, SLOTS * i + j + 1)
                        pool.wait_ge(g_msgs, SLOTS * i + j - 1)
                        pool.sem_inc(slot_turns, 1)
                        gather_group(hw_table, g_idx, g_xg, g_gathered, j)

        @block.scalar
        def _(act):
            act.dma_start(rows_i[:, :, :], dst_rows.rearrange("i (j e) -> i j e", j=SLOTS)).then_inc(rows_loaded, 16)
            act.dma_start(src_sb[:, :], src_cols).then_inc(src_loaded, 16)
            act.dma_start(dst_i[:, :], dst_cols).then_inc(dst_loaded, 16)
            act.wait_ge(bias_ready, 1)
            for c in range(CH):
                act.wait_ge(node_h, c + 1)
                w = min(QW, NP - c * QW)
                nc.scalar.activation(hidT[:, c * QW:c * QW + w], ps[:, c, 0:w], ACT.Identity, bias=b1n_lo[:, 0:1],
                                     scale=SLOPE).then_inc(node_lo, 1)
            act.wait_ge(span_found, 2)
            act.dma_start(base_dram[:, :].rearrange("a (i j) -> (a i) j", j=SLOTS), low[:, :]).then_inc(span_written, 16)
            act.dma_start(span_dram[:, :].rearrange("a (i j) -> (a i) j", j=SLOTS), high[:, :]).then_inc(span_written, 16)
            act.wait_ge(span_written, 32)
            act.dma_start(base_bc[:, :], base_dram[:, :].to_broadcast([P, GROUPS])).then_inc(span_back, 16)
            act.dma_start(span_bc[:, :], span_dram[:, :].to_broadcast([P, GROUPS])).then_inc(span_back, 16)
            act.wait_ge(node_sum, 4)
            act.dma_start(natural(xt_table), xt_sb[:, :, :]).then_inc(table_written, 16)
            act.wait_ge(src_loaded, 16)
            act.wait_ge(bias_ready, 3)

            def copy_idx(j, it, first):
                g = SLOTS * it + j
                if not first:
                    act.wait_ge(gathered[j], 16 * TILES * it)
                nc.scalar.copy(idx[:, j, :], src_sb[:, bass.ds(g * TILES, TILES)]).then_inc(idx_ready, 1)

            def copy_keys(j, it, first):
                g = SLOTS * it + j
                if not first:
                    act.wait_ge(oh_done, g - 1)
                nc.scalar.copy(keyf[:, j, :], keys[:, bass.ds(g * 3 * TILES, 3 * TILES)]).then_inc(keyf_ready, 1)

            def g_copy_key(layer, j, it, first):
                g = SLOTS * it + j
                if not first:
                    act.wait_ge(g_rel_done[layer], NWIN * (g - 1))
                nc.scalar.copy(g_key[:, j, :], g_dst[:, bass.ds(g * TILES, TILES)]).then_inc(g_key_ready[layer], 1)

            def g_load(layer):
                act.dma_start(g_src[:, :], src_cols).then_inc(g_loaded[layer], 16)
                act.dma_start(g_dst_i[:, :], dst_cols).then_inc(g_loaded[layer], 16)

            def leaky(j, it, first):
                g = SLOTS * it + j
                act.wait_ge(h_done, g + 1)
                if not first:
                    act.wait_ge(et_done, g - 1)
                z = ps_h[j].rearrange("p (a e) -> p a e", a=2)
                nc.scalar.activation(hT[:, j, 0, :, :], z, ACT.Relu, bias=b1e_up[:, 0:1], scale=1.0 - SLOPE)
                nc.scalar.activation(hT[:, j, 1, :, :], z, ACT.Identity, bias=b1e_lo[:, 0:1],
                                     scale=SLOPE).then_inc(leaky_done, 1)

            for j in range(SLOTS):
                copy_idx(j, 0, True)
            act.wait_ge(flag_made, 1)
            fast0 = nc.scalar.value_load(flags[0:1, 0:1], min_val=0, max_val=1)
            with act.If(fast0 == 1):
                for j in range(SLOTS):
                    copy_keys(j, 0, True)
                    leaky(j, 0, True)
                act.wait_ge(table_written, 16)
                w = a_words(0, ACT_BLKS)
                nc.scalar.activation(w.bitcast(F32), zero_col[:, 0:1].to_broadcast([P, w.shape[1]]), ACT.Copy).then_inc(a_zero, 1)
                with act.Fori(1, ITERS) as i:
                    for j in range(SLOTS):
                        copy_idx(j, i, False)
                        copy_keys(j, i, False)
                        leaky(j, i, False)
            with act.Else():
                g_load(0)
                act.wait_ge(g_ready[0], 1)
                for j in range(SLOTS):
                    g_copy_key(0, j, 0, True)
                    leaky(j, 0, True)
                with act.Fori(1, ITERS) as i:
                    for j in range(SLOTS):
                        copy_idx(j, i, False)
                        g_copy_key(0, j, i, False)
                        leaky(j, i, False)

            def roots(n, nb):
                act.wait_ge(stat_ready, n)
                nc.scalar.activation(stat[:, 2, 0:nb], stat[:, 1, 0:nb], ACT.Sqrt, bias=eps_sb[:, 0:1]).then_inc(root, 1)

            def part_one(q):
                b0, nb = QUART[q]
                act.wait_ge(x1t_done, q + 1)
                if q:
                    act.wait_ge(lin_done, q)
                nc.scalar.copy(x1T[:, 0:nb, :], x1t_of(nb)).then_inc(x1t_copied, 1)
                act.wait_ge(lin_done, q + 1)
                nc.scalar.copy(parts[:, b0:b0 + nb, 0, :], lin_of(nb)[:, :, 1, :]).then_inc(part_hi, 1)

            def part_two(q):
                b0, nb = QUART[q]
                act.wait_ge(part_res, q + 1)
                nc.scalar.copy(parts[:, b0:b0 + nb, 1, :], blocks_of(res, nb)).then_inc(part_mid, 1)

            for q, (b0, nb) in enumerate(QUART):
                roots(2 * q + 1, nb)
                roots(2 * q + 2, nb)
                part_one(q)
                if q:
                    part_two(q - 1)
            part_two(3)
            act.wait_ge(flag_made, 2)
            fast1 = nc.scalar.value_load(flags[0:1, 1:2], min_val=0, max_val=1)
            with act.If(fast1 == 0):
                g_load(1)
                act.wait_ge(g_table, 1)
                act.dma_start(natural(hw_table), x_sb[:, :, :]).then_inc(g_table_written, 16)
                act.wait_ge(g_ready[1], 1)

                def g_copy_idx(j, it, first):
                    if not first:
                        act.wait_ge(g_gathered[j], 16 * TILES * it)
                    nc.scalar.copy(g_idx[:, j, :], g_src[:, bass.ds((SLOTS * it + j) * TILES, TILES)]).then_inc(g_idx_ready, 1)

                for j in range(SLOTS):
                    g_copy_idx(j, 0, True)
                    g_copy_key(1, j, 0, True)
                with act.Fori(1, ITERS) as i:
                    for j in range(SLOTS):
                        g_copy_idx(j, i, False)
                        g_copy_key(1, j, i, False)
            for n in range(NBATCH):
                roots(9 + n, BATCH)

        @block.tensor
        def _(pe):
            pe.wait_ge(loaded, LOADED)
            for c in range(CH):
                w = min(QW, NP - c * QW)
                nc.tensor.matmul(ps[:, c, 0:w], w1n_sb[:, :], xT[:, c * QW:c * QW + w], start=True,
                                 stop=True).then_inc(node_h, 1)
            pe.wait_ge(node_act, CH)
            for b in range(BLKS):
                mm = nc.tensor.matmul(ps[:, b // 8, (b % 8) * D:(b % 8 + 1) * D], hidT[:, b * P:(b + 1) * P],
                                      w2n_sb[:, :], start=True, stop=True)
            mm.then_inc(node_mm, 1)
            pe.wait_ge(node_sum, 4)
            pe.wait_ge(consts, CONSTS)
            pe.wait_ge(zeroed, 1)

            def hidden(j, it, first):
                g = SLOTS * it + j
                pe.wait_ge(ea_landed[j], 16 * (it + 1))
                if not first:
                    pe.wait_ge(leaky_done, g - 1)
                for a in range(2):
                    mm = nc.tensor.matmul(ps_h[j][:, a * P:(a + 1) * P], w1e_bd[:, a, :], ea[:, j, :], start=True, stop=True)
                mm.then_inc(h_done, 1)

            def edge_rows(j, it, first):
                g = SLOTS * it + j
                if not first:
                    pe.wait_ge(msgs_done, g - 1)
                nc.tensor.matmul(ps_e[j], ones_row[:, :], b2e_row[:, :, :].rearrange("a k d -> a (k d)"), start=True, stop=False)
                pe.wait_ge(leaky_done, g + 1)
                for a in range(2):
                    for part in range(2):
                        mm = nc.tensor.matmul(ps_e[j][:, a * P:(a + 1) * P], hT[:, j, part, a, :], w2e_bd[:, :],
                                              start=False, stop=(a == 1 and part == 1))
                mm.then_inc(et_done, 1)

            def adjacency(j, it, first):
                g = SLOTS * it + j
                pe.wait_ge(oh_done, g + 1)
                if not first:
                    pe.wait_ge(a_added, g - 1)
                for k in range(TILES):
                    mm = nc.tensor.matmul(ps_a[j], oh_lo[:, j, k, :], oh_key[:, j, k, :], start=(k == 0), stop=(k == TILES - 1))
                mm.then_inc(a_done, 1)

            def sums(j, it, first):
                g = SLOTS * it + j
                pe.wait_ge(msgs_done, g + 1)
                if not first:
                    pe.wait_ge(s_added, g - 1)
                for k in range(TILES):
                    mm = nc.tensor.matmul(ps_s[j], msg[:, j, k, :], oh_rel[:, j, k, :], start=(k == 0), stop=(k == TILES - 1))
                mm.then_inc(s_done, 1)

            def g_windows(layer, rows, ready, j, it, first):
                pe.wait_ge(ready, SLOTS * it + j + 1)
                for w in range(NWIN):
                    n = NWIN * (SLOTS * it + j) + w
                    b = (NWIN * j + w) % 2
                    pe.wait_ge(g_oh_done[layer], n + 1)
                    if not (first and NWIN * j + w < 2):
                        pe.wait_ge(g_added[layer], n - 1)
                    for k in range(TILES):
                        mm = nc.tensor.matmul(ps_w[b], rows[:, j, k, :], g_oh[:, b, k, :], start=(k == 0), stop=(k == TILES - 1))
                    mm.then_inc(g_win_done[layer], 1)

            pe.wait_ge(flag_made, 1)
            fast0 = nc.tensor.value_load(flags[0:1, 0:1], min_val=0, max_val=1)
            with pe.If(fast0 == 1):
                for j in range(SLOTS):
                    hidden(j, 0, True)
                    adjacency(j, 0, True)
                    edge_rows(j, 0, True)
                    sums(j, 0, True)
                with pe.Fori(1, ITERS) as i:
                    for j in range(SLOTS):
                        hidden(j, i, False)
                        adjacency(j, i, False)
                        edge_rows(j, i, False)
                        sums(j, i, False)
            with pe.Else():
                for j in range(SLOTS):
                    hidden(j, 0, True)
                    edge_rows(j, 0, True)
                    g_windows(0, msg, msgs_done, j, 0, True)
                with pe.Fori(1, ITERS) as i:
                    for j in range(SLOTS):
                        hidden(j, i, False)
                        edge_rows(j, i, False)
                        g_windows(0, msg, msgs_done, j, i, False)

            def back(q, done, used):
                if q >= 2:
                    pe.wait_ge(used, q - 1)
                for b in range(QUART[q][0], sum(QUART[q])):
                    t = b - QUART[q][0]
                    mm = nc.tensor.transpose(ps_t[q % 2][:, t * MC:(t + 1) * MC], aggT[:, b * P:(b + 1) * P], ident[0:MC, 0:MC])
                mm.then_inc(done, 1)

            def linear(q):
                b0, nb = QUART[q]
                pe.wait_ge(x1_ready, q + 1)
                if q:
                    pe.wait_ge(x1t_copied, q)
                for t in range(nb):
                    mm = nc.tensor.transpose(x1t_of(nb)[:, t, :], x1_sb[:, b0 + t, :], ident[:, :])
                mm.then_inc(x1t_done, 1)
                pe.wait_ge(x1t_copied, q + 1)
                if q:
                    pe.wait_ge(lin_used, q)
                for t in range(nb):
                    mm = nc.tensor.matmul(lin_of(nb)[:, t, :, :], x1T[:, t, :], wab[:, :, :], start=True, stop=True)
                mm.then_inc(lin_done, 1)

            pe.wait_ge(idents, 2)
            pe.wait_ge(rest_loaded, REST)
            pe.wait_ge(sums_done, 1)
            back(0, back_done, back_used)
            back(1, back_done, back_used)
            for q in range(4):
                linear(q)
                if q < 2:
                    back(q + 2, back_done, back_used)
            pe.wait_ge(heavy_found, 4)
            nc.tensor.matmul(ps[0:1, 1, 0:BLKS], ones_col[:, :], heavy[:, :], start=True, stop=True).then_inc(heavy_counted, 1)
            pe.wait_ge(parts_ready, 4)
            pe.wait_ge(flag_made, 2)

            def neighbours(n, first):
                for t in range(BATCH):
                    if not first:
                        pe.wait_ge(near_used, BATCH * n + t - BATCH + 1)
                    for hb in range(BLKS):
                        mm = nc.tensor.matmul(ps[:, t, 0:PARTS * D], A[:, hb, bass.ds((BATCH * n + t) * P, P)],
                                              parts[:, hb, :, :].rearrange("p s d -> p (s d)"), start=(hb == 0), stop=(hb == BLKS - 1))
                    mm.then_inc(near_done, 1)

            fast1 = nc.tensor.value_load(flags[0:1, 1:2], min_val=0, max_val=1)
            with pe.If(fast1 == 1):
                neighbours(0, True)
                with pe.Fori(1, NBATCH) as n:
                    neighbours(n, False)
            with pe.Else():
                for j in range(SLOTS):
                    g_windows(1, g_msg, g_msgs, j, 0, True)
                with pe.Fori(1, ITERS) as i:
                    for j in range(SLOTS):
                        g_windows(1, g_msg, g_msgs, j, i, False)
                pe.wait_ge(g_added[1], NWIN * GROUPS)
                for q in range(4):
                    back(q, g_back, g_back_used)

        @block.vector
        def _(dve):
            links = [0]

            def link(ins):
                links[0] += 1
                ins.then_inc(chain, 1)
                dve.wait_ge(chain, links[0])

            nc.vector.memset(w1e_bd[:, :, :], 0.0)
            nc.vector.memset(w2e_bd[:, :], 0.0)
            nc.vector.memset(ones_row[:, :], 1.0)
            nc.vector.memset(ones_col[:, :], 1.0)
            nc.vector.memset(zero_col[:, :], 0.0)
            nc.vector.memset(msg[:, :, :, :], 1.0)
            nc.vector.memset(eps_sb[:, :], EPS).then_inc(zeroed, 1)
            dve.wait_ge(loaded, LOADED)
            nc.vector.tensor_scalar(b1n_lo[:, :], b1n_sb[:, :], SLOPE, None, ALU.mult).then_inc(bias_ready, 1)
            dve.wait_ge(rows_loaded, 16)
            nc.vector.tensor_reduce(low[:, :], rows_i[:, :, :], AX_X, ALU.min).then_inc(span_found, 1)
            link(nc.vector.scalar_tensor_tensor(out=rows_f[:, :, :], in0=rows_i[:, :, :], scalar=float(PAD_DST), in1=rows_i[:, :, :],
                                                op0=ALU.is_lt, op1=ALU.mult))
            nc.vector.tensor_reduce(high[:, :], rows_f[:, :, :], AX_X, ALU.max).then_inc(span_found, 1)
            for c in range(CH):
                w = min(QW, NP - c * QW)
                h = hidT[:, c * QW:c * QW + w]
                dve.wait_ge(node_lo, c + 1)
                nc.vector.scalar_tensor_tensor(out=h, in0=ps[:, c, 0:w], scalar=b1n_sb[:, 0:1], in1=h, op0=ALU.add,
                                               op1=ALU.max).then_inc(node_act, 1)
            dve.wait_ge(src_loaded, 16)
            nc.vector.tensor_scalar(hi_i[:, :], src_sb[:, :], 7, None, ALU.arith_shift_right)
            link(nc.vector.tensor_scalar(lo_i[:, :], src_sb[:, :], P - 1, None, ALU.bitwise_and))
            kv = keys[:, :].rearrange("p (g c k) -> p g c k", c=3, k=TILES)
            tiles = "p (g k) -> p g k"
            nc.vector.tensor_copy(kv[:, :, LO, :], lo_i[:, :].rearrange(tiles, k=TILES))
            dve.wait_ge(node_mm, 1)
            for q in range(4):
                nb = min(8, BLKS - 8 * q)
                nc.vector.tensor_tensor(xt_sb[:, 8 * q:8 * q + nb, :], ps[:, q, 0:nb * D].rearrange("p (b d) -> p b d", d=D),
                                        b2n_bc[:, :].rearrange("p (a d) -> p a d", a=1).to_broadcast([P, nb, D]),
                                        ALU.add).then_inc(node_sum, 1)
            dve.wait_ge(consts, CONSTS)
            nc.vector.tensor_scalar(b1e_lo[:, :], b1e_sb[:, :], SLOPE, None, ALU.mult).then_inc(bias_ready, 1)
            nc.vector.tensor_scalar(b1e_up[:, :], b1e_sb[:, :], 1.0 - SLOPE, None, ALU.mult).then_inc(bias_ready, 1)
            dve.wait_ge(dst_loaded, 16)
            dve.wait_ge(span_back, 32)
            link(nc.vector.tensor_copy(dst_f[:, :], dst_i[:, :]))
            link(nc.vector.tensor_tensor(kv[:, :, REL, :], dst_f[:, :].rearrange(tiles, k=TILES),
                                         base_bc[:, :].rearrange("p (g a) -> p g a", a=1).to_broadcast([P, GROUPS, TILES]), ALU.subtract))
            nc.vector.scalar_tensor_tensor(out=kv[:, :, KEY, :], in0=hi_i[:, :].rearrange(tiles, k=TILES), scalar=float(SPAN),
                                           in1=kv[:, :, REL, :], op0=ALU.mult, op1=ALU.add)
            nc.vector.tensor_copy(base_i[:, :], base_bc[0:1, :])
            link(nc.vector.tensor_tensor(span_bc[:, :], span_bc[:, :], base_bc[:, :], ALU.subtract))
            link(nc.vector.tensor_reduce(widest[:, :], span_bc[:, :], AX_X, ALU.max))
            link(nc.vector.tensor_scalar(flags[:, 0:1], widest[:, :], float(SPAN), None, ALU.is_lt))
            dve.wait_ge(iotas, 2)
            nc.vector.memset(aggT[:, :], 0.0)
            link(nc.vector.memset(a_words(EARLY_BLKS, POOL_BLKS), 0))
            nc.vector.sem_inc(flag_made, 1)

            def messages(j, it):
                g = SLOTS * it + j
                dve.wait_ge(et_done, g + 1)
                dve.wait_ge(gathered[j], 16 * TILES * (it + 1))
                nc.vector.tensor_tensor(msg[:, j, :, 0:D], ps_e[j].rearrange("p (k d) -> p k d", d=D), xg[:, j, :, :],
                                        ALU.mult).then_inc(msgs_done, 1)

            def one_hots(j, it, first):
                g = SLOTS * it + j
                dve.wait_ge(keyf_ready, g + 1)
                if not first:
                    dve.wait_ge(a_done, g - 1)
                    dve.wait_ge(s_done, g - 1)
                kf = keyf[:, j, :].rearrange("p (c k) -> p c k", c=3)
                for k in range(TILES):
                    nc.vector.tensor_scalar(oh_lo[:, j, k, :], iota_k[:, 0:P], kf[:, LO, k:k + 1], None, ALU.is_equal)
                    nc.vector.tensor_scalar(oh_key[:, j, k, :], iota_k[:, 0:KEYS], kf[:, KEY, k:k + 1], None, ALU.is_equal)
                nc.vector.tensor_tensor(oh_rel[:, j, :, :], iota_s[:, :].rearrange("p (a s) -> p a s", a=1).to_broadcast([P, TILES, SPAN]),
                                        kf[:, REL, :].rearrange("p (k a) -> p k a", a=1).to_broadcast([P, TILES, SPAN]),
                                        ALU.is_equal).then_inc(oh_done, 1)

            def add_windows(j, it, first):
                g = SLOTS * it + j
                base = dve.value_load(base_i[0:1, bass.ds(g, 1)], min_val=0, max_val=N - 1)
                dve.wait_ge(a_done, g + 1)
                if not first:
                    dve.wait_ge(a_added, g)
                win = A[:, :, bass.ds(base, SPAN)]
                nc.vector.tensor_tensor(win, ps_a[j].rearrange("p (b s) -> p b s", s=SPAN), win, ALU.add).then_inc(a_added, 1)
                dve.wait_ge(s_done, g + 1)
                if not first:
                    dve.wait_ge(s_added, g)
                seg = aggT[:, bass.ds(base, SPAN)]
                nc.vector.tensor_tensor(seg, ps_s[j], seg, ALU.add).then_inc(s_added, 1)

            def g_window_sums(layer, j, it, first):
                g = SLOTS * it + j
                dve.wait_ge(g_key_ready[layer], g + 1)
                for w in range(NWIN):
                    n = NWIN * g + w
                    b = (NWIN * j + w) % 2
                    nc.vector.tensor_scalar(g_rel[:, b, :], g_key[:, j, :], float(-w * WINDOW), None, ALU.add).then_inc(g_rel_done[layer], 1)
                    dve.wait_ge(g_rel_done[layer], n + 1)
                    if not (first and NWIN * j + w < 2):
                        dve.wait_ge(g_win_done[layer], n - 1)
                    for k in range(TILES):
                        ins = nc.vector.tensor_scalar(g_oh[:, b, k, :], g_iota[:, :], g_rel[:, b, k:k + 1], None, ALU.is_equal)
                    ins.then_inc(g_oh_done[layer], 1)
                    dve.wait_ge(g_win_done[layer], n + 1)
                    seg = aggT[:, w * WINDOW:(w + 1) * WINDOW]
                    if not (first and j == 0):
                        dve.wait_ge(g_added[layer], n - NWIN + 1)
                    nc.vector.tensor_tensor(seg, ps_w[b], seg, ALU.add).then_inc(g_added[layer], 1)

            def g_setup(layer):
                dve.wait_ge(g_loaded[layer], 32)
                nc.vector.tensor_copy(g_iota[:, :], iota_k[:, 0:WINDOW])
                nc.vector.tensor_copy(g_dst[:, :], g_dst_i[:, :]).then_inc(g_ready[layer], 1)

            fast0 = dve.value_load(flags[0:1, 0:1], min_val=0, max_val=1)
            with dve.If(fast0 == 1):
                dve.wait_ge(table_written, 16)
                nc.vector.memset(a_words(ACT_BLKS, EARLY_BLKS), 0).then_inc(a_zero, 1)
                for j in range(SLOTS):
                    one_hots(j, 0, True)
                    messages(j, 0)
                    if j == 0:
                        dve.wait_ge(a_zero, 3)
                    add_windows(j, 0, j == 0)
                with dve.Fori(1, ITERS) as i:
                    for j in range(SLOTS):
                        one_hots(j, i, False)
                        messages(j, i)
                        add_windows(j, i, False)
                dve.wait_ge(a_added, GROUPS)
                dve.wait_ge(s_added, GROUPS)
            with dve.Else():
                g_setup(0)
                for j in range(SLOTS):
                    messages(j, 0)
                    g_window_sums(0, j, 0, True)
                with dve.Fori(1, ITERS) as i:
                    for j in range(SLOTS):
                        dve.wait_ge(g_win_done[0], NWIN * (SLOTS * i + j - 1))
                        messages(j, i)
                        g_window_sums(0, j, i, False)
                dve.wait_ge(g_added[0], NWIN * GROUPS)
            nc.vector.sem_inc(sums_done, 1)

            def row(ap, nb):
                return ap.rearrange("p (a d) -> p a d", a=1).to_broadcast([P, nb, D])

            def col(ap, nb):
                return ap.rearrange("p (b a) -> p b a", a=1).to_broadcast([P, nb, D])

            norms = [0]

            def layernorm(y, nb):
                norms[0] += 1
                s = blocks_of(sq, nb)
                link(nc.vector.tensor_reduce(stat[:, 0, 0:nb], y, AX_X, ALU.add))
                link(nc.vector.tensor_scalar(stat[:, 0, 0:nb], stat[:, 0, 0:nb], 1.0 / D, None, ALU.mult))
                link(nc.vector.tensor_tensor(y, y, col(stat[:, 0, 0:nb], nb), ALU.subtract))
                link(nc.vector.tensor_tensor(s, y, y, ALU.mult))
                link(nc.vector.tensor_reduce(stat[:, 1, 0:nb], s, AX_X, ALU.add))
                nc.vector.tensor_scalar(stat[:, 1, 0:nb], stat[:, 1, 0:nb], 1.0 / D, None, ALU.mult).then_inc(stat_ready, 1)
                dve.wait_ge(root, norms[0])
                link(nc.vector.reciprocal(stat[:, 3, 0:nb], stat[:, 2, 0:nb]))
                link(nc.vector.tensor_tensor(y, y, col(stat[:, 3, 0:nb], nb), ALU.mult))

            def rows_of_layer0(q):
                b0, nb = QUART[q]
                y, x = x1_sb[:, b0:b0 + nb, :], x_sb[:, b0:b0 + nb, :]
                v = back_of(q, nb)
                deg = v[:, :, D:MC]
                rd = rdeg[:, b0:b0 + nb].rearrange("p (b a) -> p b a", a=1)
                dve.wait_ge(back_done, q + 1)
                nc.vector.tensor_scalar(heavy[:, b0:b0 + nb].rearrange("p (b a) -> p b a", a=1), deg, float(MAX_COUNT), None,
                                        ALU.is_gt).then_inc(heavy_found, 1)
                link(nc.vector.tensor_scalar(rd, deg, 1.0, None, ALU.max))
                nc.vector.reciprocal(rd, rd)
                link(nc.vector.scalar_tensor_tensor(out=y, in0=v[:, :, 0:D], scalar=scl[:, 0:1], in1=x, op0=ALU.mult, op1=ALU.add))
                nc.vector.sem_inc(back_used, 1)
                layernorm(y, nb)
                link(nc.vector.tensor_tensor(y, y, row(gam_bc[:, :], nb), ALU.mult))
                link(nc.vector.tensor_tensor(y, y, row(bet_bc[:, :], nb), ALU.add))
                link(nc.vector.tensor_tensor(y, y, x, ALU.add))
                layernorm(y, nb)
                nc.vector.sem_inc(x1_ready, 1)

            def parts_of(q):
                b0, nb = QUART[q]
                y = x1_sb[:, b0:b0 + nb, :]
                lin = lin_of(nb)
                r = blocks_of(res, nb)
                dve.wait_ge(part_hi, q + 1)
                nc.vector.tensor_tensor(r, lin[:, :, 1, :], parts[:, b0:b0 + nb, 0, :], ALU.subtract).then_inc(part_res, 1)
                link(nc.vector.tensor_tensor(y, lin[:, :, 0, :], y, ALU.add))
                nc.vector.sem_inc(lin_used, 1)
                link(nc.vector.tensor_tensor(y, y, row(b1_bc[:, :], nb), ALU.add))
                dve.wait_ge(part_mid, q + 1)
                link(nc.vector.tensor_tensor(parts[:, b0:b0 + nb, 2, :], r, parts[:, b0:b0 + nb, 1, :], ALU.subtract))
                nc.vector.sem_inc(parts_ready, 1)

            dve.wait_ge(rest_loaded, REST)
            link(nc.vector.tensor_tensor(scl[:, :], rw_bc[:, 0:1], rw_bc[:, 1:2], ALU.mult))
            dve.wait_ge(x_back, 16)
            for q in range(4):
                rows_of_layer0(q)
                if q:
                    parts_of(q - 1)
            dve.wait_ge(heavy_counted, 1)
            link(nc.vector.tensor_reduce(n_heavy[:, :], ps[0:1, 1, 0:BLKS], AX_X, ALU.add))
            link(nc.vector.scalar_tensor_tensor(out=flags[0:1, 1:2], in0=n_heavy[:, :], scalar=0.0, in1=flags[0:1, 0:1],
                                                op0=ALU.is_equal, op1=ALU.mult))
            nc.vector.sem_inc(flag_made, 1)
            parts_of(3)

            def finish(n):
                b0 = n * BATCH
                y = x_sb[:, b0:b0 + BATCH, :]
                link(nc.vector.tensor_tensor(y, y, col(rdeg[:, b0:b0 + BATCH], BATCH), ALU.mult))
                link(nc.vector.tensor_tensor(y, y, x1_sb[:, b0:b0 + BATCH, :], ALU.add))
                layernorm(y, BATCH)
                nc.vector.sem_inc(out_ready, 1)

            fast1 = dve.value_load(flags[0:1, 1:2], min_val=0, max_val=1)
            before, norm0 = links[0], norms[0]
            with dve.If(fast1 == 1):
                for n in range(NBATCH):
                    for t in range(BATCH):
                        b = n * BATCH + t
                        dve.wait_ge(near_done, b + 1)
                        ins = nc.vector.tensor_reduce(x_sb[:, b, :], ps[:, t, 0:PARTS * D].rearrange("p (s d) -> p d s", d=D), AX_X,
                                                      ALU.add)
                        if t < BATCH - 1:
                            ins.then_inc(near_used, 1)
                        else:
                            ins.then_inc(near_used, 1)
                            dve.wait_ge(near_used, b + 1)
                    finish(n)
            with dve.Else():
                links[0], norms[0] = before, norm0
                link(nc.vector.tensor_tensor(x_sb[:, :, :], parts[:, :, 0, :], parts[:, :, 1, :], ALU.add))
                link(nc.vector.tensor_tensor(x_sb[:, :, :], x_sb[:, :, :], parts[:, :, 2, :], ALU.add))
                nc.vector.sem_inc(g_table, 1)
                nc.vector.memset(g_msg[:, :, :, :], 1.0)
                link(nc.vector.memset(aggT[:, :], 0.0))
                g_setup(1)

                def rows_passed(j, it):
                    g = SLOTS * it + j
                    dve.wait_ge(g_gathered[j], 16 * TILES * (it + 1))
                    nc.vector.tensor_copy(g_msg[:, j, :, 0:D], g_xg[:, j, :, :]).then_inc(g_msgs, 1)

                for j in range(SLOTS):
                    rows_passed(j, 0)
                    g_window_sums(1, j, 0, True)
                with dve.Fori(1, ITERS) as i:
                    for j in range(SLOTS):
                        dve.wait_ge(g_win_done[1], NWIN * (SLOTS * i + j - 1))
                        rows_passed(j, i)
                        g_window_sums(1, j, i, False)
                for q, (b0, nb) in enumerate(QUART):
                    dve.wait_ge(g_back, q + 1)
                    link(nc.vector.tensor_copy(x_sb[:, b0:b0 + nb, :], back_of(q, nb)[:, :, 0:D]))
                    nc.vector.sem_inc(g_back_used, 1)
                for n in range(NBATCH):
                    finish(n)


def kernel(x, src, dst, edge_attr_32, L0_gnn_W1n, L0_gnn_b1n, L0_gnn_W2n, L0_gnn_b2n, L0_gnn_W1e, L0_gnn_b1e,
           L0_gnn_W2e, L0_gnn_b2e, L0_gnn_res_w, L0_gnn_dp_scale, L0_gnn_gamma, L0_gnn_beta, L1_gnn_W, L1_gnn_b):
    import numpy as np
    import concourse.bacc as bacc
    from concourse import mybir as _mybir
    from concourse.bass_utils import run_bass_kernel_spmd

    x, src, dst, edges = (np.asarray(a) for a in (x, src, dst, edge_attr_32))
    N, D = x.shape
    E, FE = edges.shape
    n_pad = up(N, P) * P
    groups = up(up(E, GROUP), SLOTS) * SLOTS
    e_pad = groups * GROUP

    x_pad = np.zeros((n_pad, D), x.dtype)
    x_pad[:N] = x
    src_pad = np.zeros(e_pad, src.dtype)
    src_pad[:E] = src
    dst_pad = np.full(e_pad, PAD_DST, dst.dtype)
    dst_pad[:E] = dst
    ea_pad = np.zeros((e_pad, FE), edges.dtype)
    ea_pad[:E] = edges
    ea_t = np.ascontiguousarray(ea_pad.reshape(groups, TILES, P, FE).transpose(1, 3, 0, 2).reshape(TILES * FE, groups * P))
    arrays = {
        "x_nat": x_pad, "x_t": np.ascontiguousarray(x_pad.T),
        "src_cols": np.ascontiguousarray(src_pad.reshape(-1, P).T),
        "dst_rows": dst_pad.reshape(-1, SLOTS * GROUP),
        "dst_cols": np.ascontiguousarray(dst_pad.reshape(-1, P).T),
        "ea_t": ea_t,
        "W1n": L0_gnn_W1n, "b1n": L0_gnn_b1n, "W2n": L0_gnn_W2n, "b2n": L0_gnn_b2n,
        "W1e": L0_gnn_W1e, "b1e": L0_gnn_b1e, "W2e": L0_gnn_W2e, "b2e": L0_gnn_b2e,
        "res_w": L0_gnn_res_w, "dp_scale": L0_gnn_dp_scale, "gamma": L0_gnn_gamma, "beta": L0_gnn_beta,
        "W1_t": np.ascontiguousarray(np.asarray(L1_gnn_W).T), "b1": L1_gnn_b,
    }
    arrays = {k: np.ascontiguousarray(v) for k, v in arrays.items()}
    nc = bacc.Bacc("TRN2", target_bir_lowering=False, num_devices=1)
    args = [nc.dram_tensor(k, a.shape, _mybir.dt.from_np(a.dtype), kind="ExternalInput").ap() for k, a in arrays.items()]
    args.append(nc.dram_tensor("out", (N, D), F32, kind="ExternalOutput").ap())
    gnn_kernel(nc, *args)
    r = run_bass_kernel_spmd(nc, [arrays], core_ids=[0])
    return r.results[0]["out"]
```

```python
from contextlib import ExitStack

import concourse.bass as bass
from concourse import mybir

F32 = mybir.dt.float32
F16 = mybir.dt.float16
BF16 = mybir.dt.bfloat16
U32 = mybir.dt.uint32
I32 = mybir.dt.int32
ALU = mybir.AluOpType
ACT = mybir.ActivationFunctionType
AX_X = mybir.AxisListType.X

P = 128
EPS = 1e-5
SLOPE = 0.1
TILES = 4
GROUP = TILES * P
SLOTS = 2
RING = 4
SPAN = 20
WARM = 8
WINDOW = 448
PAD_DST = 1 << 14
MAX_COUNT = 256
PARTS = 3


def up(n, m):
    return -(-n // m)


def wait_from(eng, sem, count):
    if not isinstance(count, int) or count > 0:
        eng.wait_ge(sem, count)


def gnn_kernel(nc, n_edges, x_nat, x_t, src_cols, dst_rows, dst_cols, ea_t, W1n, b1n, W2n, b2n, W1e, b1e, W2e, b2e,
               res_w, dp_scale, gamma, beta, W1_t, b1, out):
    N, D = out.shape
    H = W1n.shape[1]
    FE = W1e.shape[0]
    HE = W1e.shape[1]
    BLKS = up(N, P)
    NP = BLKS * P
    GROUPS = src_cols.shape[1] // TILES
    ITERS = GROUPS // SLOTS
    LAST = up(n_edges, P) - (GROUPS - 1) * TILES
    LOOPS = GROUPS // RING - 1
    NWIN = up(N, WINDOW)
    MC = D + 1
    KEYS = BLKS * SPAN
    CB = 4
    CH = up(BLKS, CB)
    TABLE_PARTS = (CH + 1) // 2
    CHUNKS = [(CB * c, min(CB, BLKS - CB * c)) for c in range(CH)]
    BATCH = 5
    NBATCH = BLKS // BATCH
    PIECES = [(BATCH * n, BATCH) for n in range(NBATCH - 1)] + [(BLKS - BATCH, BATCH - 1), (BLKS - 1, 1)]
    LO, KEY, REL = range(3)
    FIRST_NODES = (CH + 1) // 2 * CB * P
    assert 0 < LAST <= TILES and CH % 2 == 1 and NBATCH * BATCH == BLKS and KEYS <= 512 and NWIN * WINDOW <= NP

    with ExitStack() as ctx:
        def sem(name):
            return ctx.enter_context(nc.semaphore(name))

        def alloc(scope):
            return lambda name, shape, dt=F32: scope.enter_context(nc.sbuf_tensor(name, shape, dt))

        xt_table = nc.dram_tensor("xt_table", [NP, D], F32, kind="Internal")
        hw_table = nc.dram_tensor("hw_table", [NP, D], F32, kind="Internal")
        base_dram = nc.dram_tensor("base_dram", [1, GROUPS], F32, kind="Internal")
        span_dram = nc.dram_tensor("span_dram", [1, GROUPS], F32, kind="Internal")

        sb = alloc(ctx)
        w1e_bd = sb("w1e_bd", [P, 2, P])
        w2e_bd = sb("w2e_bd", [P, P])
        b2e_rows = sb("b2e_rows", [PARTS, TILES, D], BF16)
        ones_row = sb("ones_row", [PARTS, P], BF16)
        ones_col = sb("ones_col", [P, 1])
        b1e_sb = sb("b1e_sb", [P, 1])
        b1e_up = sb("b1e_up", [P, 1])
        b1e_lo = sb("b1e_lo", [P, 1])
        b2n_bc = sb("b2n_bc", [P, D])
        gam_bc = sb("gam_bc", [P, D])
        bet_bc = sb("bet_bc", [P, D])
        b1_bc = sb("b1_bc", [P, D])
        rw_bc = sb("rw_bc", [P, 2])
        scl = sb("scl", [P, 1])
        wab = sb("wab", [D, 2, D])
        ident = sb("ident", [P, P])
        eps_sb = sb("eps_sb", [P, 1])
        iota_k = sb("iota_k", [P, 512], F16)
        iota_s = sb("iota_s", [P, SPAN])
        flags = sb("flags", [P, 2], I32)
        zero_col = sb("zero_col", [P, 1])
        unused = sb("unused", [P, 1])
        aggT = sb("aggT", [MC, NP])

        early = ExitStack()
        eb = alloc(early)
        xT = eb("xT", [D, NP])
        hidT = eb("hidT", [H, NP])
        xt_sb = eb("xt_sb", [P, BLKS, D])
        rows_i = eb("rows_i", [ITERS, SLOTS, GROUP], I32)
        rows_f = eb("rows_f", [ITERS, SLOTS, GROUP])
        w1n_sb = eb("w1n_sb", [D, H])
        w2n_sb = eb("w2n_sb", [H, D])
        b1n_sb = eb("b1n_sb", [H, 1])
        b1n_lo = eb("b1n_lo", [H, 1])
        dst_i = eb("dst_i", [P, GROUPS * TILES], I32)
        low = eb("low", [ITERS, SLOTS])
        high = eb("high", [ITERS, SLOTS])
        base_bc = eb("base_bc", [P, GROUPS])
        span_bc = eb("span_bc", [P, GROUPS])
        widest = eb("widest", [P, 1])
        b2e_sb = eb("b2e_sb", [PARTS, TILES, D])
        b2e_hi = eb("b2e_hi", [PARTS, TILES, D], BF16)
        b2e_mid = eb("b2e_mid", [PARTS, TILES, D], BF16)
        b2e_lo = eb("b2e_lo", [PARTS, TILES, D], BF16)
        hi_i = eb("hi_i", [P, GROUPS * TILES], I32)
        lo_i = eb("lo_i", [P, GROUPS * TILES], I32)

        g_src = eb("g_src", [P, GROUPS * TILES], I32)
        g_dst = eb("g_dst", [P, GROUPS * TILES])
        g_dst_i = eb("g_dst_i", [P, GROUPS * TILES], I32)
        g_iota = eb("g_iota", [P, WINDOW])
        g_key = eb("g_key", [P, SLOTS, TILES])
        g_rel = eb("g_rel", [P, 2, TILES])
        g_oh = eb("g_oh", [P, 2, TILES, WINDOW])
        g_idx = eb("g_idx", [P, RING, TILES], I32)
        g_xg = eb("g_xg", [P, RING, TILES, D])
        g_msg = eb("g_msg", [P, SLOTS, TILES, MC])
        early.close()

        A = sb("A", [P, BLKS, NP], BF16)
        EARLY_BLKS = 9
        ACT_BLKS = 2
        MLP_BLKS = 2 * NP * 4 // (NP * 2)
        ROW_BLKS = (2 * NP * 4 + BLKS * D * 4 + 2 * SLOTS * GROUP * 4) // (NP * 2)
        assert 4 * (2 * NP + BLKS * D + 2 * SLOTS * GROUP + 3 * GROUPS * TILES + 2 * GROUPS + H + D + 10 * D + 16) <= EARLY_BLKS * NP * 2

        loop = ExitStack()
        lb = alloc(loop)
        src_sb = lb("src_sb", [P, GROUPS * TILES], I32)
        keys = lb("keys", [P, GROUPS * 3 * TILES], F16)
        base_i = lb("base_i", [1, GROUPS], I32)
        idx = lb("idx", [P, RING, TILES], I32)
        keyf = lb("keyf", [P, SLOTS, 3 * TILES])
        ea = lb("ea", [P, RING, P])
        hT = lb("hT", [P, SLOTS, 2, 2, P])
        xg = lb("xg", [P, RING, TILES, D])
        msg = lb("msg", [P, SLOTS, TILES, MC])
        oh_lo = lb("oh_lo", [P, SLOTS, TILES, P], BF16)
        oh_key = lb("oh_key", [P, SLOTS, TILES, KEYS], BF16)
        oh_rel = lb("oh_rel", [P, SLOTS, TILES, SPAN])
        loop.close()

        tb = alloc(ctx)
        x_sb = tb("x_sb", [P, BLKS, D])
        x1_sb = tb("x1_sb", [P, BLKS, D])
        parts = tb("parts", [P, BLKS, PARTS, D], BF16)
        sq = tb("sq", [P, 2, BATCH, D])
        res = tb("res", [P, BATCH, D])
        x1T = tb("x1T", [D, BATCH, P])
        stat = tb("stat", [P, 2, 4, BATCH])
        rdeg = tb("rdeg", [P, BLKS])
        heavy = tb("heavy", [P, BLKS])
        n_heavy = tb("n_heavy", [1, 1])
        X_FIRST = BATCH * (GROUPS * TILES // (BATCH * D))

        ps = ctx.enter_context(nc.psum_tensor("ps", [P, 8, 512], F32))
        ps_h = [ps[:, j, 0:2 * P] for j in range(SLOTS)]
        ps_e = [ps[:, 2 + j, 0:TILES * D] for j in range(SLOTS)]
        ps_a = [ps[:, 4 + j, 0:KEYS] for j in range(SLOTS)]
        ps_s = [ps[0:MC, 6 + j, 0:SPAN] for j in range(SLOTS)]
        ps_w = [ps[0:MC, 4 + j, 0:WINDOW] for j in range(2)]
        ps_t = [ps[:, 6 + j, :] for j in range(2)]
        EARLY_PAIRS = 4
        LATER_ROWS = (0, 10, 15, 20)
        NEAR_BANKS = (0, 1, 6, 7, 2, 3, 4, 5)

        zeroed = sem("zeroed")
        consts = sem("consts")
        first_loaded = sem("first_loaded")
        second_loaded = sem("second_loaded")
        rest_loaded = sem("rest_loaded")
        src_loaded = sem("src_loaded")
        dst_loaded = sem("dst_loaded")
        rows_loaded = sem("rows_loaded")
        iotas = sem("iotas")
        idents = sem("idents")
        bias_ready = sem("bias_ready")
        node_h = sem("node_h")
        node_lo = sem("node_lo")
        node_act = sem("node_act")
        node_mm = sem("node_mm")
        node_sum = sem("node_sum")
        table_written = sem("table_written")
        span_found = sem("span_found")
        span_written = sem("span_written")
        span_back = sem("span_back")
        flag_made = sem("flag_made")
        a_zero = sem("a_zero")
        slot_turns = sem("slot_turns")
        idx_ready = sem("idx_ready")
        keyf_ready = sem("keyf_ready")
        ea_landed = [sem(f"ea_landed{j}") for j in range(RING)]
        gathered = [sem(f"gathered{j}") for j in range(RING)]
        h_done = sem("h_done")
        leaky_done = sem("leaky_done")
        et_done = sem("et_done")
        msgs_done = sem("msgs_done")
        oh_done = sem("oh_done")
        a_done = sem("a_done")
        a_added = sem("a_added")
        s_done = sem("s_done")
        s_added = sem("s_added")
        sums_done = sem("sums_done")
        g_loaded = [sem(f"g_loaded{l}") for l in range(2)]
        g_ready = [sem(f"g_ready{l}") for l in range(2)]
        g_key_ready = [sem(f"g_key_ready{l}") for l in range(2)]
        g_rel_done = [sem(f"g_rel_done{l}") for l in range(2)]
        g_oh_done = [sem(f"g_oh_done{l}") for l in range(2)]
        g_win_done = [sem(f"g_win_done{l}") for l in range(2)]
        g_added = [sem(f"g_added{l}") for l in range(2)]
        g_table = sem("g_table")
        g_table_written = sem("g_table_written")
        g_gathered = [sem(f"g_gathered{j}") for j in range(RING)]
        g_idx_ready = sem("g_idx_ready")
        g_msgs = sem("g_msgs")
        g_back = sem("g_back")
        g_back_used = sem("g_back_used")
        chain = sem("chain")
        pool_chain = sem("pool_chain")
        summed = sem("summed")
        squared = sem("squared")
        normed = sem("normed")
        rows_mixed = sem("rows_mixed")
        root_added = sem("root_added")
        bias_added = sem("bias_added")
        x_first_back = sem("x_first_back")
        x_back = sem("x_back")
        back_done = sem("back_done")
        back_used = sem("back_used")
        stat_ready = sem("stat_ready")
        root = sem("root")
        x1_ready = sem("x1_ready")
        x1t_done = sem("x1t_done")
        x1t_copied = sem("x1t_copied")
        lin_done = sem("lin_done")
        root_weights = sem("root_weights")
        part_hi = sem("part_hi")
        part_res = sem("part_res")
        part_mid = sem("part_mid")
        parts_ready = sem("parts_ready")
        heavy_found = sem("heavy_found")
        heavy_counted = sem("heavy_counted")
        near_done = sem("near_done")
        near_used = sem("near_used")
        out_ready = sem("out_ready")
        out_written = sem("out_written")

        block = ctx.enter_context(nc.Block())

        def row(ap, nb=BATCH):
            return ap.rearrange("p (a d) -> p a d", a=1).to_broadcast([P, nb, D])

        def a_words(b0, b1):
            return A[:, b0:b1, :].rearrange("p b n -> p (b n)").bitcast(U32)

        CONSTS = 16 * 9
        REST = 16 * 7

        def steps(eng, step):
            for g in range(RING):
                step(g, g, 0)
            with eng.Fori(1, LOOPS) as i:
                for j in range(RING):
                    step(RING * i + j, j, i)
            for g in range(RING * LOOPS, GROUPS):
                step(g, g % RING, g // RING)

        def exists(g):
            return not isinstance(g, int) or g < GROUPS

        def tiles_of(g):
            return LAST if isinstance(g, int) and g == GROUPS - 1 else TILES

        def row_of(v, n):
            return v.rearrange("(a d) -> a d", a=1).to_broadcast([P, n])

        def natural(table):
            return table[:, :].rearrange("(b p) d -> p b d", p=P)

        def lin_of():
            return ps[:, 4:6, :].rearrange("p a n -> p (a n)")[:, 0:BATCH * 2 * D].rearrange("p (b h d) -> p b h d", h=2, d=D)

        def x1t_of():
            return ps[0:D, 2:4, :].rearrange("p a n -> p (a n)")[:, 0:BATCH * P].rearrange("p (b n) -> p b n", n=P)

        def near_of(b):
            half = (b % 2) * 256
            return ps[:, NEAR_BANKS[b // 2 % len(NEAR_BANKS)], half:half + PARTS * D]

        def blocks_of(pair):
            return range(2 * pair, min(2 * pair + 2, BLKS))

        def x1_of(n):
            return x1_sb[:, n * BATCH:(n + 1) * BATCH, :] if 0 <= n < NBATCH else None

        def back_of(n):
            return ps_t[n % 2][:, 0:BATCH * MC].rearrange("p (b c) -> p b c", c=MC)

        @block.sync
        def _(sp):
            sp.dma_start(w1n_sb[:, :], W1n).then_inc(first_loaded, 16)
            sp.dma_start(b1n_sb[:, :], b1n.rearrange("(h a) -> h a", a=1)).then_inc(first_loaded, 16)
            sp.dma_start(xT[:, 0:FIRST_NODES], x_t[:, 0:FIRST_NODES]).then_inc(first_loaded, 16)
            sp.dma_start(w2n_sb[:, :], W2n).then_inc(second_loaded, 16)
            sp.dma_start(b2n_bc[:, :], row_of(b2n, D)).then_inc(second_loaded, 16)
            sp.dma_start(xT[:, FIRST_NODES:NP], x_t[:, FIRST_NODES:NP]).then_inc(second_loaded, 16)
            sp.dma_start(src_sb[:, :], src_cols).then_inc(src_loaded, 16)
            sp.dma_start(dst_i[:, :], dst_cols).then_inc(dst_loaded, 16)
            sp.wait_ge(zeroed, 1)
            for q in range(4):
                sp.dma_start(w1e_bd[q * FE:(q + 1) * FE, q // 2, (q % 2) * HE:(q % 2 + 1) * HE], W1e).then_inc(consts, 16)
            for q in range(2):
                sp.dma_start(w2e_bd[q * HE:(q + 1) * HE, q * D:(q + 1) * D], W2e).then_inc(consts, 16)
                sp.dma_start(b1e_sb[q * HE:(q + 1) * HE, :], b1e.rearrange("(h a) -> h a", a=1)).then_inc(consts, 16)
            sp.dma_start(b2e_sb[:, :, :], b2e.rearrange("(a k d) -> a k d", a=1, k=1).to_broadcast([PARTS, TILES, D])).then_inc(consts, 16)
            for j in range(RING):
                sp.dma_start(ea[:, j, :], ea_t[:, j * P:(j + 1) * P]).then_inc(ea_landed[j], 16)
            sp.wait_ge(span_found, 2)
            sp.dma_start(base_dram[:, :].rearrange("a (i j) -> (a i) j", j=SLOTS), low[:, :]).then_inc(span_written, 16)
            sp.dma_start(span_dram[:, :].rearrange("a (i j) -> (a i) j", j=SLOTS), high[:, :]).then_inc(span_written, 16)
            sp.wait_ge(span_written, 32)
            sp.dma_start(base_bc[:, :], base_dram[:, :].to_broadcast([P, GROUPS])).then_inc(span_back, 16)
            sp.dma_start(span_bc[:, :], span_dram[:, :].to_broadcast([P, GROUPS])).then_inc(span_back, 16)
            sp.dma_start(gam_bc[:, :], row_of(gamma, D)).then_inc(rest_loaded, 16)
            sp.dma_start(bet_bc[:, :], row_of(beta, D)).then_inc(rest_loaded, 16)
            sp.dma_start(b1_bc[:, :], row_of(b1, D)).then_inc(rest_loaded, 16)
            sp.dma_start(rw_bc[:, 0:1], row_of(res_w, 1)).then_inc(rest_loaded, 16)
            sp.dma_start(rw_bc[:, 1:2], row_of(dp_scale, 1)).then_inc(rest_loaded, 16)
            for half in range(2):
                sp.dma_start(wab[:, half, :], W1_t[half * D:(half + 1) * D, :]).then_inc(rest_loaded, 16)

            def load_ahead(g, j, turn):
                if exists(g + RING):
                    sp.wait_ge(h_done, g + 1)
                    sp.dma_start(ea[:, j, :], ea_t[:, bass.ds((g + RING) * P, P)]).then_inc(ea_landed[j], 16)

            steps(sp, load_ahead)
            sp.wait_ge(idx_ready, GROUPS)
            sp.dma_start(x_sb[:, 0:X_FIRST, :], x_nat[0:X_FIRST * P, :].rearrange("(b p) d -> p b d", p=P)).then_inc(x_first_back, 16)
            sp.wait_ge(sums_done, 1)
            sp.dma_start(x_sb[:, X_FIRST:BLKS, :], x_nat[X_FIRST * P:NP, :].rearrange("(b p) d -> p b d", p=P)).then_inc(x_back, 16)
            for n, (b0, nb) in enumerate(PIECES):
                sp.wait_ge(out_ready, n + 1)
                whole = min(nb, N // P - b0)
                if whole:
                    sp.dma_start(out[b0 * P:(b0 + whole) * P, :].rearrange("(b p) d -> p b d", p=P),
                                 x_sb[:, b0:b0 + whole, :]).then_inc(out_written, 16)
                if whole < nb:
                    full = (b0 + whole) * P
                    sp.dma_start(out[full:N, :], x_sb[0:N - full, b0 + whole, :]).then_inc(out_written, 16)
            sp.wait_ge(out_written, 16 * len(PIECES))

        def gather_group(table, index, rows, landed, g, j):
            for k in range(tiles_of(g)):
                nc.gpsimd.indirect_dma_start(
                    out=rows[:, j, k, :], out_offset=None, in_=table[:, :],
                    in_offset=bass.IndirectOffsetOnAxis(ap=index[:, j, k:k + 1], axis=0)).then_inc(landed[j], 16)

        @block.gpsimd
        def _(pool):
            links = [0]

            def pool_link(ins):
                links[0] += 1
                ins.then_inc(pool_chain, 1)
                pool.wait_ge(pool_chain, links[0])

            nc.gpsimd.iota(iota_k[:, :], pattern=[[1, 512]], base=0, channel_multiplier=0,
                           allow_small_or_imprecise_dtypes=True).then_inc(iotas, 1)
            nc.gpsimd.iota(iota_s[:, :], pattern=[[1, SPAN]], base=0, channel_multiplier=0,
                           allow_small_or_imprecise_dtypes=True).then_inc(iotas, 1)
            nc.gpsimd.memset(ident[:, :], 0.0).then_inc(idents, 1)
            pool.wait_ge(idents, 1)
            nc.gpsimd.affine_select(out=ident[:, :], in_=ident[:, :], compare_op=ALU.not_equal, fill=1.0,
                                    base=0, pattern=[[-1, P]], channel_multiplier=1).then_inc(idents, 1)
            nc.gpsimd.memset(a_words(EARLY_BLKS, BLKS - ACT_BLKS), 0).then_inc(a_zero, 1)
            pool.wait_ge(table_written, 16 * TABLE_PARTS)

            def gather(g, j, turn):
                pool.wait_ge(idx_ready, g + 1)
                wait_from(pool, msgs_done, g - RING + 1)
                pool.sem_inc(slot_turns, 1)
                gather_group(xt_table, idx, xg, gathered, g, j)

            steps(pool, gather)
            pool.wait_ge(rest_loaded, REST)
            for n in range(NBATCH + 2):
                if n < NBATCH:
                    y = x1_of(n)
                    pool.wait_ge(normed, n + 1)
                    pool_link(nc.gpsimd.tensor_tensor(y, y, row(gam_bc[:, :]), ALU.mult))
                    pool_link(nc.gpsimd.tensor_tensor(y, y, row(bet_bc[:, :]), ALU.add))
                    nc.gpsimd.tensor_tensor(y, y, x_sb[:, n * BATCH:(n + 1) * BATCH, :], ALU.add).then_inc(rows_mixed, 1)
                if n >= 2:
                    y = x1_of(n - 2)
                    pool.wait_ge(root_added, n - 1)
                    nc.gpsimd.tensor_tensor(y, y, row(b1_bc[:, :]), ALU.add).then_inc(bias_added, 1)
            pool.wait_ge(flag_made, 2)
            fast = nc.gpsimd.value_load(flags[0:1, 1:2], min_val=0, max_val=1)
            with pool.If(fast == 0):
                pool.wait_ge(g_table_written, 16)

                def g_gather(g, j, turn):
                    pool.wait_ge(g_idx_ready, g + 1)
                    wait_from(pool, g_msgs, g - RING + 1)
                    pool.sem_inc(slot_turns, 1)
                    gather_group(hw_table, g_idx, g_xg, g_gathered, g, j)

                steps(pool, g_gather)

        @block.scalar
        def _(act):
            def clear(words):
                nc.scalar.activation(words.bitcast(F32), zero_col[:, 0:1].to_broadcast([P, words.shape[1]]), ACT.Copy).then_inc(a_zero, 1)

            act.dma_start(rows_i[:, :, :], dst_rows.rearrange("i (j e) -> i j e", j=SLOTS)).then_inc(rows_loaded, 16)
            act.wait_ge(zeroed, 1)
            clear(a_words(BLKS - ACT_BLKS, BLKS))
            act.wait_ge(bias_ready, 1)

            def write_table(first, last):
                b0, b1 = CHUNKS[first][0], sum(CHUNKS[last])
                act.wait_ge(node_sum, last + 1)
                act.dma_start(natural(xt_table)[:, b0:b1, :], xt_sb[:, b0:b1, :]).then_inc(table_written, 16)

            for c, (b0, nb) in enumerate(CHUNKS):
                act.wait_ge(node_h, c + 1)
                nc.scalar.activation(hidT[:, b0 * P:(b0 + nb) * P], ps[:, c, 0:nb * P], ACT.Identity, bias=b1n_lo[:, 0:1],
                                     scale=SLOPE).then_inc(node_lo, 1)
                if c >= 4 and c % 2 == 0:
                    write_table(c - 4, c - 3)
            write_table(CH - 3, CH - 2)
            write_table(CH - 1, CH - 1)
            act.wait_ge(src_loaded, 16)
            act.wait_ge(bias_ready, 3)

            def copy_idx(g, j, turn):
                wait_from(act, gathered[j], 16 * TILES * turn)
                nc.scalar.copy(idx[:, j, :], src_sb[:, bass.ds(g * TILES, TILES)]).then_inc(idx_ready, 1)

            def copy_keys(g, s):
                wait_from(act, oh_done, g - 1)
                nc.scalar.copy(keyf[:, s, :], keys[:, bass.ds(g * 3 * TILES, 3 * TILES)]).then_inc(keyf_ready, 1)

            def g_copy_key(layer, g, s):
                wait_from(act, g_rel_done[layer], NWIN * (g - 1))
                nc.scalar.copy(g_key[:, s, :], g_dst[:, bass.ds(g * TILES, TILES)]).then_inc(g_key_ready[layer], 1)

            def g_load(layer):
                act.dma_start(g_src[:, :], src_cols).then_inc(g_loaded[layer], 16)
                act.dma_start(g_dst_i[:, :], dst_cols).then_inc(g_loaded[layer], 16)

            def leaky(g, s):
                act.wait_ge(h_done, g + 1)
                wait_from(act, et_done, g - 1)
                z = ps_h[s].rearrange("p (a e) -> p a e", a=2)
                nc.scalar.activation(hT[:, s, 0, :, :], z, ACT.Relu, bias=b1e_up[:, 0:1], scale=1.0 - SLOPE)
                nc.scalar.activation(hT[:, s, 1, :, :], z, ACT.Identity, bias=b1e_lo[:, 0:1],
                                     scale=SLOPE).then_inc(leaky_done, 1)

            for j in range(RING):
                copy_idx(j, j, 0)
            act.wait_ge(node_mm, CH)
            act.wait_ge(node_act, CH)
            clear(a_words(0, MLP_BLKS))
            act.wait_ge(flag_made, 1)
            fast0 = nc.scalar.value_load(flags[0:1, 0:1], min_val=0, max_val=1)
            with act.If(fast0 == 1):
                for g in range(SLOTS):
                    copy_keys(g, g)
                    leaky(g, g)
                act.wait_ge(table_written, 16 * TABLE_PARTS)
                act.wait_ge(span_found, 2)
                clear(a_words(MLP_BLKS, ROW_BLKS))

                def ahead(g, j, turn):
                    if exists(g + RING):
                        copy_idx(g + RING, j, turn + 1)
                    if exists(g + SLOTS):
                        copy_keys(g + SLOTS, j % SLOTS)
                        leaky(g + SLOTS, j % SLOTS)

                steps(act, ahead)
            with act.Else():
                act.wait_ge(a_zero, 3)
                g_load(0)
                act.wait_ge(g_ready[0], 1)

                def g_ahead(g, j, turn):
                    g_copy_key(0, g, j % SLOTS)
                    leaky(g, j % SLOTS)
                    if exists(g + RING):
                        copy_idx(g + RING, j, turn + 1)

                steps(act, g_ahead)

            def squares(count, which, y, nb=BATCH):
                act.wait_ge(summed, count)
                nc.scalar.activation(sq[:, which, 0:nb, :], y, ACT.Square).then_inc(squared, 1)

            def roots(count, which, nb=BATCH):
                act.wait_ge(stat_ready, count)
                nc.scalar.activation(stat[:, which, 2, 0:nb], stat[:, which, 1, 0:nb], ACT.Sqrt, bias=eps_sb[:, 0:1],
                                     scale=1.0 / D).then_inc(root, 1)

            def x1_transposed(n):
                act.wait_ge(x1t_done, n + 1)
                wait_from(act, lin_done, n)
                nc.scalar.copy(x1T[:, :, :], x1t_of()).then_inc(x1t_copied, 1)

            def part_one(n):
                act.wait_ge(lin_done, n + 1)
                nc.scalar.copy(parts[:, n * BATCH:(n + 1) * BATCH, 0, :], lin_of()[:, :, 1, :]).then_inc(part_hi, 1)

            def part_two(n):
                act.wait_ge(part_res, n + 1)
                nc.scalar.copy(parts[:, n * BATCH:(n + 1) * BATCH, 1, :], res[:, :, :]).then_inc(part_mid, 1)
                nc.scalar.copy(x1_of(n), lin_of()[:, :, 0, :]).then_inc(root_added, 1)

            nc.scalar.activation(unused[:, :], eps_sb[:, :], ACT.Sqrt)
            for n in range(NBATCH + 2):
                first, second, last = n < NBATCH, 1 <= n <= NBATCH, n >= 2
                count = (n if n < 1 else 2 * n - 1)
                rows, before = x1_of(n), x1_of(n - 1)
                if first:
                    squares(count + 1, 0, rows)
                if second:
                    squares(count + first + 1, 1, before)
                if first:
                    roots(count + 1, 0)
                if last:
                    part_one(n - 2)
                if second:
                    roots(count + first + 1, 1)
                if last:
                    part_two(n - 2)
                if second:
                    x1_transposed(n - 1)
            act.wait_ge(flag_made, 2)
            fast1 = nc.scalar.value_load(flags[0:1, 1:2], min_val=0, max_val=1)
            with act.If(fast1 == 0):
                act.wait_ge(near_done, EARLY_PAIRS)
                g_load(1)
                act.wait_ge(g_table, 1)
                act.dma_start(natural(hw_table), x_sb[:, :, :]).then_inc(g_table_written, 16)
                act.wait_ge(g_ready[1], 1)

                def g_copies(g, j, turn):
                    wait_from(act, g_gathered[j], 16 * TILES * turn)
                    nc.scalar.copy(g_idx[:, j, :], g_src[:, bass.ds(g * TILES, TILES)]).then_inc(g_idx_ready, 1)
                    g_copy_key(1, g, j % SLOTS)

                steps(act, g_copies)
            for n, (b0, nb) in enumerate(PIECES):
                squares(2 * NBATCH + n + 1, 0, x_sb[:, b0:b0 + nb, :], nb)
                roots(2 * NBATCH + n + 1, 0, nb)

        @block.tensor
        def _(pe):
            pe.wait_ge(zeroed, 1)
            ones = msg[:, :, :, :].rearrange("p s k c -> p (s k c)")
            for _ in range(WARM):
                nc.tensor.matmul(ps[:, 7, 0:2 * P], ones[:, 0:P], ones[:, 0:2 * P], start=True, stop=True)

            def node_hidden(c):
                b0, nb = CHUNKS[c]
                nc.tensor.matmul(ps[:, c, 0:nb * P], w1n_sb[:, :], xT[:, b0 * P:(b0 + nb) * P], start=True,
                                 stop=True).then_inc(node_h, 1)

            def node_rows(c):
                b0, nb = CHUNKS[c]
                pe.wait_ge(node_act, c + 1)
                for t in range(nb):
                    mm = nc.tensor.matmul(ps[:, c, t * D:(t + 1) * D], hidT[:, (b0 + t) * P:(b0 + t + 1) * P], w2n_sb[:, :],
                                          start=True, stop=True)
                mm.then_inc(node_mm, 1)

            pe.wait_ge(first_loaded, 16 * 3)
            for c in range(CH + 2):
                if c == 2:
                    pe.wait_ge(second_loaded, 16 * 3)
                if c < CH:
                    node_hidden(c)
                if c >= 2:
                    node_rows(c - 2)
            pe.wait_ge(node_sum, CH)
            pe.wait_ge(consts, CONSTS)
            pe.wait_ge(zeroed, 1)
            pe.wait_ge(bias_ready, 4)

            def hidden(g, j, turn):
                sl = j % SLOTS
                pe.wait_ge(ea_landed[j], 16 * (turn + 1))
                wait_from(pe, leaky_done, g - 1)
                for a in range(2):
                    mm = nc.tensor.matmul(ps_h[sl][:, a * P:(a + 1) * P], w1e_bd[:, a, :], ea[:, j, :], start=True, stop=True)
                mm.then_inc(h_done, 1)

            def edge_rows(g, sl):
                wait_from(pe, msgs_done, g - 1)
                nc.tensor.matmul(ps_e[sl], ones_row[:, :], b2e_rows[:, :, :].rearrange("a k d -> a (k d)"), start=True, stop=False)
                pe.wait_ge(leaky_done, g + 1)
                for a in range(2):
                    for part in range(2):
                        mm = nc.tensor.matmul(ps_e[sl][:, a * P:(a + 1) * P], hT[:, sl, part, a, :], w2e_bd[:, :],
                                              start=False, stop=(a == 1 and part == 1))
                mm.then_inc(et_done, 1)

            def adjacency(g, sl):
                pe.wait_ge(oh_done, g + 1)
                wait_from(pe, a_added, g - 1)
                for k in range(TILES):
                    mm = nc.tensor.matmul(ps_a[sl], oh_lo[:, sl, k, :], oh_key[:, sl, k, :], start=(k == 0), stop=(k == TILES - 1))
                mm.then_inc(a_done, 1)

            def sums(g, sl):
                pe.wait_ge(msgs_done, g + 1)
                wait_from(pe, s_added, g - 1)
                for k in range(TILES):
                    mm = nc.tensor.matmul(ps_s[sl], msg[:, sl, k, :], oh_rel[:, sl, k, :], start=(k == 0), stop=(k == TILES - 1))
                mm.then_inc(s_done, 1)

            def g_windows(layer, rows, ready, g, sl):
                pe.wait_ge(ready, g + 1)
                for w in range(NWIN):
                    n = NWIN * g + w
                    b = (NWIN * sl + w) % 2
                    pe.wait_ge(g_oh_done[layer], n + 1)
                    wait_from(pe, g_added[layer], n - 1)
                    for k in range(TILES):
                        mm = nc.tensor.matmul(ps_w[b], rows[:, sl, k, :], g_oh[:, b, k, :], start=(k == 0), stop=(k == TILES - 1))
                    mm.then_inc(g_win_done[layer], 1)

            pe.wait_ge(flag_made, 1)
            fast0 = nc.tensor.value_load(flags[0:1, 0:1], min_val=0, max_val=1)
            with pe.If(fast0 == 1):
                hidden(0, 0, 0)
                hidden(1, 1, 0)
                edge_rows(0, 0)
                adjacency(0, 0)

                def step(g, j, turn):
                    sl, nx = j % SLOTS, (j + 1) % SLOTS
                    if exists(g + 1):
                        edge_rows(g + 1, nx)
                    sums(g, sl)
                    if exists(g + 1):
                        adjacency(g + 1, nx)
                    if exists(g + 2):
                        hidden(g + 2, (j + 2) % RING, turn + (j + 2) // RING)

                steps(pe, step)
            with pe.Else():
                def g_step(g, j, turn):
                    hidden(g, j, turn)
                    edge_rows(g, j % SLOTS)
                    g_windows(0, msg, msgs_done, g, j % SLOTS)

                steps(pe, g_step)

            def back(n, done, used):
                if n >= 2:
                    pe.wait_ge(used, n - 1)
                for t in range(BATCH):
                    b = n * BATCH + t
                    mm = nc.tensor.transpose(ps_t[n % 2][:, t * MC:(t + 1) * MC], aggT[:, b * P:(b + 1) * P], ident[0:MC, 0:MC])
                mm.then_inc(done, 1)

            def linear(n):
                pe.wait_ge(x1_ready, n + 1)
                wait_from(pe, x1t_copied, n)
                for t in range(BATCH):
                    mm = nc.tensor.transpose(x1t_of()[:, t, :], x1_sb[:, n * BATCH + t, :], ident[:, :])
                mm.then_inc(x1t_done, 1)
                pe.wait_ge(x1t_copied, n + 1)
                wait_from(pe, root_added, n)
                wait_from(pe, part_res, n)
                for t in range(BATCH):
                    mm = nc.tensor.matmul(lin_of()[:, t, :, :], x1T[:, t, :], wab[:, :, :], start=True, stop=True)
                mm.then_inc(lin_done, 1)

            pe.wait_ge(idents, 2)
            pe.wait_ge(root_weights, 1)
            pe.wait_ge(sums_done, 1)
            for n in range(3):
                back(n, back_done, back_used)
            def neighbours(pair, h0, h1):
                for b in blocks_of(pair):
                    for hb in range(h0, h1):
                        mm = nc.tensor.matmul(near_of(b), A[:, hb, b * P:(b + 1) * P], parts[:, hb, :, :].rearrange("p s d -> p (s d)"),
                                              start=(hb == 0 and b == 2 * pair), stop=(hb == BLKS - 1 and b == blocks_of(pair)[-1]))
                return mm

            def rows(counts):
                for n in range(NBATCH):
                    if n == NBATCH - 2:
                        pe.wait_ge(heavy_found, NBATCH)
                        pe.wait_ge(x1t_copied, n)
                        nc.tensor.matmul(ps[0:1, 3, 256:256 + BLKS], ones_col[:, :], heavy[:, :], start=True,
                                         stop=True).then_inc(heavy_counted, 1)
                    linear(n)
                    if n + 3 < NBATCH:
                        back(n + 3, back_done, back_used)
                    if counts and n:
                        pe.wait_ge(parts_ready, n)
                        for pair in range(2):
                            neighbours(pair, (n - 1) * BATCH, n * BATCH)
                    if counts and n >= 2:
                        pe.wait_ge(back_used, NBATCH)
                        for pair in range(2, EARLY_PAIRS):
                            neighbours(pair, LATER_ROWS[n - 2], LATER_ROWS[n - 1])
                if counts:
                    pe.wait_ge(parts_ready, NBATCH)
                    for pair in range(EARLY_PAIRS):
                        neighbours(pair, (NBATCH - 1) * BATCH, BLKS).then_inc(near_done, 1)

            fast0 = nc.tensor.value_load(flags[0:1, 0:1], min_val=0, max_val=1)
            with pe.If(fast0 == 1):
                rows(True)
            with pe.Else():
                rows(False)
                pe.sem_inc(near_done, EARLY_PAIRS)
            pe.wait_ge(root_added, NBATCH)
            pe.wait_ge(flag_made, 2)
            fast1 = nc.tensor.value_load(flags[0:1, 1:2], min_val=0, max_val=1)
            with pe.If(fast1 == 1):
                for pair in range(EARLY_PAIRS, up(BLKS, 2)):
                    wait_from(pe, near_used, 2 * (pair - len(NEAR_BANKS) + 1))
                    neighbours(pair, 0, BLKS).then_inc(near_done, 1)
            with pe.Else():
                def g_step(g, j, turn):
                    g_windows(1, g_msg, g_msgs, g, j % SLOTS)

                steps(pe, g_step)
                pe.wait_ge(g_added[1], NWIN * GROUPS)
                for n in range(NBATCH):
                    back(n, g_back, g_back_used)

        @block.vector
        def _(dve):
            links = [0]

            def link(ins):
                links[0] += 1
                ins.then_inc(chain, 1)
                dve.wait_ge(chain, links[0])

            nc.vector.memset(w1e_bd[:, :, :], 0.0)
            nc.vector.memset(w2e_bd[:, :], 0.0)
            nc.vector.memset(ones_row[:, :], 1.0)
            nc.vector.memset(ones_col[:, :], 1.0)
            nc.vector.memset(zero_col[:, :], 0.0)
            nc.vector.memset(msg[:, :, :, :], 1.0)
            nc.vector.memset(eps_sb[:, :], EPS).then_inc(zeroed, 1)
            nc.vector.memset(aggT[:, :], 0.0)
            dve.wait_ge(rows_loaded, 16)
            nc.vector.tensor_reduce(low[:, :], rows_i[:, :, :], AX_X, ALU.min).then_inc(span_found, 1)
            link(nc.vector.scalar_tensor_tensor(out=rows_f[:, :, :], in0=rows_i[:, :, :], scalar=float(PAD_DST), in1=rows_i[:, :, :],
                                                op0=ALU.is_lt, op1=ALU.mult))
            dve.wait_ge(first_loaded, 16 * 3)
            nc.vector.tensor_scalar(b1n_lo[:, :], b1n_sb[:, :], SLOPE, None, ALU.mult).then_inc(bias_ready, 1)
            nc.vector.tensor_reduce(high[:, :], rows_f[:, :, :], AX_X, ALU.max).then_inc(span_found, 1)

            def node_leaky(c):
                b0, nb = CHUNKS[c]
                h = hidT[:, b0 * P:(b0 + nb) * P]
                dve.wait_ge(node_lo, c + 1)
                nc.vector.scalar_tensor_tensor(out=h, in0=ps[:, c, 0:nb * P], scalar=b1n_sb[:, 0:1], in1=h, op0=ALU.add,
                                               op1=ALU.max).then_inc(node_act, 1)

            def node_bias(c):
                b0, nb = CHUNKS[c]
                dve.wait_ge(node_mm, c + 1)
                nc.vector.tensor_tensor(xt_sb[:, b0:b0 + nb, :], ps[:, c, 0:nb * D].rearrange("p (b d) -> p b d", d=D),
                                        row(b2n_bc[:, :], nb), ALU.add).then_inc(node_sum, 1)

            for c in range(CH + 2):
                if c < CH:
                    node_leaky(c)
                if c == 2:
                    dve.wait_ge(second_loaded, 16 * 3)
                if c >= 2:
                    node_bias(c - 2)
            dve.wait_ge(src_loaded, 16)
            nc.vector.tensor_scalar(hi_i[:, :], src_sb[:, :], 7, None, ALU.arith_shift_right)
            link(nc.vector.tensor_scalar(lo_i[:, :], src_sb[:, :], P - 1, None, ALU.bitwise_and))
            kv = keys[:, :].rearrange("p (g c k) -> p g c k", c=3, k=TILES)
            tiles = "p (g k) -> p g k"
            nc.vector.tensor_copy(kv[:, :, LO, :], lo_i[:, :].rearrange(tiles, k=TILES))
            dve.wait_ge(consts, CONSTS)
            nc.vector.tensor_scalar(b1e_lo[:, :], b1e_sb[:, :], SLOPE, None, ALU.mult).then_inc(bias_ready, 1)
            nc.vector.tensor_scalar(b1e_up[:, :], b1e_sb[:, :], 1.0 - SLOPE, None, ALU.mult).then_inc(bias_ready, 1)
            dve.wait_ge(idents, 2)
            link(nc.vector.tensor_copy(b2e_hi[:, :, :], b2e_sb[:, :, :]))
            link(nc.vector.tensor_tensor(b2e_sb[:, :, :], b2e_sb[:, :, :], b2e_hi[:, :, :], ALU.subtract))
            link(nc.vector.tensor_copy(b2e_mid[:, :, :], b2e_sb[:, :, :]))
            link(nc.vector.tensor_tensor(b2e_lo[:, :, :], b2e_sb[:, :, :], b2e_mid[:, :, :], ALU.subtract))
            link(nc.vector.tensor_scalar(b2e_rows[:, :, :], b2e_hi[:, :, :], ident[0:PARTS, 0:1], None, ALU.mult))
            link(nc.vector.scalar_tensor_tensor(out=b2e_rows[:, :, :], in0=b2e_mid[:, :, :], scalar=ident[0:PARTS, 1:2],
                                                in1=b2e_rows[:, :, :], op0=ALU.mult, op1=ALU.add))
            nc.vector.scalar_tensor_tensor(out=b2e_rows[:, :, :], in0=b2e_lo[:, :, :], scalar=ident[0:PARTS, 2:3],
                                           in1=b2e_rows[:, :, :], op0=ALU.mult, op1=ALU.add).then_inc(bias_ready, 1)
            dve.wait_ge(dst_loaded, 16)
            dve.wait_ge(span_back, 32)
            link(nc.vector.tensor_tensor(kv[:, :, REL, :], dst_i[:, :].rearrange(tiles, k=TILES),
                                         base_bc[:, :].rearrange("p (g a) -> p g a", a=1).to_broadcast([P, GROUPS, TILES]), ALU.subtract))
            nc.vector.scalar_tensor_tensor(out=kv[:, :, KEY, :], in0=hi_i[:, :].rearrange(tiles, k=TILES), scalar=float(SPAN),
                                           in1=kv[:, :, REL, :], op0=ALU.mult, op1=ALU.add)
            nc.vector.tensor_copy(base_i[:, :], base_bc[0:1, :])
            link(nc.vector.tensor_tensor(span_bc[:, :], span_bc[:, :], base_bc[:, :], ALU.subtract))
            link(nc.vector.tensor_reduce(widest[:, :], span_bc[:, :], AX_X, ALU.max))
            link(nc.vector.tensor_scalar(flags[:, 0:1], widest[:, :], float(SPAN), None, ALU.is_lt))
            dve.wait_ge(iotas, 2)
            nc.vector.sem_inc(flag_made, 1)

            def messages(g, j, turn):
                sl = j % SLOTS
                dve.wait_ge(et_done, g + 1)
                dve.wait_ge(gathered[j], 16 * TILES * turn + 16 * tiles_of(g))
                if fast:
                    wait_from(dve, s_done, g - 1)
                else:
                    wait_from(dve, g_win_done[0], NWIN * (g - 1))
                nc.vector.tensor_tensor(msg[:, sl, :, 0:D], ps_e[sl].rearrange("p (k d) -> p k d", d=D), xg[:, j, :, :],
                                        ALU.mult).then_inc(msgs_done, 1)

            def one_hots(g, sl):
                dve.wait_ge(keyf_ready, g + 1)
                wait_from(dve, a_done, g - 1)
                wait_from(dve, s_done, g - 1)
                kf = keyf[:, sl, :].rearrange("p (c k) -> p c k", c=3)
                for k in range(TILES):
                    nc.vector.tensor_scalar(oh_lo[:, sl, k, :], iota_k[:, 0:P], kf[:, LO, k:k + 1], None, ALU.is_equal)
                    nc.vector.tensor_scalar(oh_key[:, sl, k, :], iota_k[:, 0:KEYS], kf[:, KEY, k:k + 1], None, ALU.is_equal)
                nc.vector.tensor_tensor(oh_rel[:, sl, :, :], iota_s[:, :].rearrange("p (a s) -> p a s", a=1).to_broadcast([P, TILES, SPAN]),
                                        kf[:, REL, :].rearrange("p (k a) -> p k a", a=1).to_broadcast([P, TILES, SPAN]),
                                        ALU.is_equal).then_inc(oh_done, 1)

            def add_windows(g, sl):
                base = dve.value_load(base_i[0:1, bass.ds(g, 1)], min_val=0, max_val=N - 1)
                dve.wait_ge(a_done, g + 1)
                wait_from(dve, a_added, g)
                win = A[:, :, bass.ds(base, SPAN)]
                nc.vector.tensor_tensor(win, ps_a[sl].rearrange("p (b s) -> p b s", s=SPAN), win, ALU.add).then_inc(a_added, 1)
                dve.wait_ge(s_done, g + 1)
                wait_from(dve, s_added, g)
                seg = aggT[:, bass.ds(base, SPAN)]
                nc.vector.tensor_tensor(seg, ps_s[sl], seg, ALU.add).then_inc(s_added, 1)

            def g_window_sums(layer, g, sl):
                dve.wait_ge(g_key_ready[layer], g + 1)
                for w in range(NWIN):
                    n = NWIN * g + w
                    b = (NWIN * sl + w) % 2
                    nc.vector.tensor_scalar(g_rel[:, b, :], g_key[:, sl, :], float(-w * WINDOW), None, ALU.add).then_inc(g_rel_done[layer], 1)
                    dve.wait_ge(g_rel_done[layer], n + 1)
                    wait_from(dve, g_win_done[layer], n - 1)
                    for k in range(TILES):
                        ins = nc.vector.tensor_scalar(g_oh[:, b, k, :], g_iota[:, :], g_rel[:, b, k:k + 1], None, ALU.is_equal)
                    ins.then_inc(g_oh_done[layer], 1)
                    dve.wait_ge(g_win_done[layer], n + 1)
                    seg = aggT[:, w * WINDOW:(w + 1) * WINDOW]
                    wait_from(dve, g_added[layer], n - NWIN + 1)
                    nc.vector.tensor_tensor(seg, ps_w[b], seg, ALU.add).then_inc(g_added[layer], 1)

            def g_setup(layer):
                dve.wait_ge(g_loaded[layer], 32)
                nc.vector.tensor_copy(g_iota[:, :], iota_k[:, 0:WINDOW])
                nc.vector.tensor_copy(g_dst[:, :], g_dst_i[:, :]).then_inc(g_ready[layer], 1)

            fast0 = dve.value_load(flags[0:1, 0:1], min_val=0, max_val=1)
            with dve.If(fast0 == 1):
                nc.vector.memset(a_words(ROW_BLKS, EARLY_BLKS), 0).then_inc(a_zero, 1)
                fast = True
                one_hots(0, 0)

                def step(g, j, turn):
                    messages(g, j, turn)
                    if exists(g + 1):
                        one_hots(g + 1, (j + 1) % SLOTS)
                    if isinstance(g, int) and g == 0:
                        dve.wait_ge(a_zero, 5)
                    add_windows(g, j % SLOTS)

                steps(dve, step)
                dve.wait_ge(a_added, GROUPS)
                dve.wait_ge(s_added, GROUPS)
            with dve.Else():
                fast = False
                g_setup(0)

                def g_step(g, j, turn):
                    messages(g, j, turn)
                    g_window_sums(0, g, j % SLOTS)

                steps(dve, g_step)
                dve.wait_ge(g_added[0], NWIN * GROUPS)
            nc.vector.sem_inc(sums_done, 1)

            def col(ap, nb=BATCH):
                return ap.rearrange("p (b a) -> p b a", a=1).to_broadcast([P, nb, D])

            def mark(ins):
                links[0] += 1
                ins.then_inc(chain, 1)
                return links[0]

            norms = [0]

            def norm_sum(y, which, ready, nb=BATCH):
                dve.wait_ge(chain, ready)
                return mark(nc.vector.tensor_reduce(stat[:, which, 0, 0:nb], y, AX_X, ALU.add))

            def norm_centre(y, which, ready, nb=BATCH):
                dve.wait_ge(chain, ready)
                norms[0] += 1
                nc.vector.scalar_tensor_tensor(out=y, in0=col(stat[:, which, 0, 0:nb], nb), scalar=-1.0 / D, in1=y,
                                               op0=ALU.mult, op1=ALU.add).then_inc(summed, 1)
                return norms[0]

            def norm_spread(which, norm, nb=BATCH):
                dve.wait_ge(squared, norm)
                nc.vector.tensor_reduce(stat[:, which, 1, 0:nb], sq[:, which, 0:nb, :], AX_X, ALU.add).then_inc(stat_ready, 1)

            def norm_inverse(which, norm, nb=BATCH):
                dve.wait_ge(root, norm)
                return mark(nc.vector.reciprocal(stat[:, which, 3, 0:nb], stat[:, which, 2, 0:nb]))

            def norm_scale(y, which, ready, nb=BATCH):
                dve.wait_ge(chain, ready)
                return nc.vector.tensor_tensor(y, y, col(stat[:, which, 3, 0:nb], nb), ALU.mult)

            def residual(n):
                b0 = n * BATCH
                v = back_of(n)
                deg = v[:, :, D:MC]
                rd = rdeg[:, b0:b0 + BATCH].rearrange("p (b a) -> p b a", a=1)
                dve.wait_ge(back_done, n + 1)
                nc.vector.tensor_scalar(heavy[:, b0:b0 + BATCH].rearrange("p (b a) -> p b a", a=1), deg, float(MAX_COUNT), None,
                                        ALU.is_gt).then_inc(heavy_found, 1)
                clamped = mark(nc.vector.tensor_scalar(rd, deg, 1.0, None, ALU.max))
                dve.wait_ge(x_first_back, 16)
                if b0 + BATCH > X_FIRST:
                    dve.wait_ge(x_back, 16)
                y = mark(nc.vector.scalar_tensor_tensor(out=x1_sb[:, b0:b0 + BATCH, :], in0=v[:, :, 0:D], scalar=scl[:, 0:1],
                                                        in1=x_sb[:, b0:b0 + BATCH, :], op0=ALU.mult, op1=ALU.add))
                dve.wait_ge(chain, clamped)
                nc.vector.reciprocal(rd, rd).then_inc(back_used, 1)
                return y

            def part_rest(n):
                dve.wait_ge(part_hi, n + 1)
                wait_from(dve, parts_ready, n)
                nc.vector.tensor_tensor(res[:, :, :], lin_of()[:, :, 1, :], parts[:, n * BATCH:(n + 1) * BATCH, 0, :],
                                        ALU.subtract).then_inc(part_res, 1)

            def part_last(n):
                dve.wait_ge(part_mid, n + 1)
                nc.vector.tensor_tensor(parts[:, n * BATCH:(n + 1) * BATCH, 2, :], res[:, :, :],
                                        parts[:, n * BATCH:(n + 1) * BATCH, 1, :], ALU.subtract).then_inc(parts_ready, 1)

            dve.wait_ge(rest_loaded, REST)
            nc.vector.tensor_tensor(wab[:, 0, :], wab[:, 0, :], ident[0:D, 0:D], ALU.add).then_inc(root_weights, 1)
            link(nc.vector.tensor_tensor(scl[:, :], rw_bc[:, 0:1], rw_bc[:, 1:2], ALU.mult))
            for n in range(NBATCH + 2):
                first, second, last = n < NBATCH, 1 <= n <= NBATCH, n >= 2
                rows, before = x1_of(n), x1_of(n - 1)
                if first:
                    added = residual(n)
                    sum0 = norm_sum(rows, 0, added)
                if second:
                    dve.wait_ge(rows_mixed, n)
                    sum1 = norm_sum(before, 1, links[0])
                if first:
                    norm0 = norm_centre(rows, 0, sum0)
                if second:
                    norm1 = norm_centre(before, 1, sum1)
                if first:
                    norm_spread(0, norm0)
                    norm_scale(rows, 0, norm_inverse(0, norm0)).then_inc(normed, 1)
                if second:
                    norm_spread(1, norm1)
                if n == NBATCH - 1:
                    dve.wait_ge(heavy_counted, 1)
                    link(nc.vector.tensor_reduce(n_heavy[:, :], ps[0:1, 3, 256:256 + BLKS], AX_X, ALU.add))
                    link(nc.vector.scalar_tensor_tensor(out=flags[0:1, 1:2], in0=n_heavy[:, :], scalar=0.0, in1=flags[0:1, 0:1],
                                                        op0=ALU.is_equal, op1=ALU.mult))
                    nc.vector.sem_inc(flag_made, 1)
                if last:
                    part_rest(n - 2)
                if second:
                    norm_scale(before, 1, norm_inverse(1, norm1)).then_inc(x1_ready, 1)
                if last:
                    part_last(n - 2)
            dve.wait_ge(bias_added, NBATCH)

            def finish(b0, nb, ready):
                y = x_sb[:, b0:b0 + nb, :]
                norm = norm_centre(y, 0, norm_sum(y, 0, ready, nb), nb)
                norm_spread(0, norm, nb)
                norm_scale(y, 0, norm_inverse(0, norm, nb), nb).then_inc(out_ready, 1)

            fast1 = dve.value_load(flags[0:1, 1:2], min_val=0, max_val=1)
            links_before, norms_before = links[0], norms[0]
            with dve.If(fast1 == 1):
                for b0, nb in PIECES:
                    for b in range(b0, b0 + nb):
                        dve.wait_ge(near_done, b // 2 + 1)
                        reduced = mark(nc.vector.tensor_reduce(x_sb[:, b, :], near_of(b).rearrange("p (s d) -> p d s", d=D),
                                                               AX_X, ALU.add))
                        dve.wait_ge(chain, reduced)
                        nc.vector.sem_inc(near_used, 1)
                        meant = mark(nc.vector.scalar_tensor_tensor(out=x_sb[:, b, :], in0=x_sb[:, b, :], scalar=rdeg[:, b:b + 1],
                                                                    in1=x1_sb[:, b, :], op0=ALU.mult, op1=ALU.add))
                    finish(b0, nb, meant)
            with dve.Else():
                links[0], norms[0] = links_before, norms_before
                link(nc.vector.tensor_tensor(x_sb[:, :, :], parts[:, :, 0, :], parts[:, :, 1, :], ALU.add))
                link(nc.vector.tensor_tensor(x_sb[:, :, :], x_sb[:, :, :], parts[:, :, 2, :], ALU.add))
                nc.vector.sem_inc(g_table, 1)
                dve.wait_ge(near_done, EARLY_PAIRS)
                nc.vector.memset(g_msg[:, :, :, :], 1.0)
                link(nc.vector.memset(aggT[:, :], 0.0))
                g_setup(1)

                def rows_passed(g, j, turn):
                    dve.wait_ge(g_gathered[j], 16 * TILES * turn + 16 * tiles_of(g))
                    wait_from(dve, g_win_done[1], NWIN * (g - 1))
                    nc.vector.tensor_copy(g_msg[:, j % SLOTS, :, 0:D], g_xg[:, j, :, :]).then_inc(g_msgs, 1)
                    g_window_sums(1, g, j % SLOTS)

                steps(dve, rows_passed)
                for n in range(NBATCH):
                    dve.wait_ge(g_back, n + 1)
                    link(nc.vector.tensor_tensor(x_sb[:, n * BATCH:(n + 1) * BATCH, :], back_of(n)[:, :, 0:D],
                                                 col(rdeg[:, n * BATCH:(n + 1) * BATCH]), ALU.mult))
                    nc.vector.sem_inc(g_back_used, 1)
                link(nc.vector.tensor_tensor(x_sb[:, :, :], x_sb[:, :, :], x1_sb[:, :, :], ALU.add))
                for b0, nb in PIECES:
                    finish(b0, nb, links[0])


def kernel(x, src, dst, edge_attr_32, L0_gnn_W1n, L0_gnn_b1n, L0_gnn_W2n, L0_gnn_b2n, L0_gnn_W1e, L0_gnn_b1e,
           L0_gnn_W2e, L0_gnn_b2e, L0_gnn_res_w, L0_gnn_dp_scale, L0_gnn_gamma, L0_gnn_beta, L1_gnn_W, L1_gnn_b):
    import numpy as np
    import concourse.bacc as bacc
    from concourse import mybir as _mybir
    from concourse.bass_utils import run_bass_kernel_spmd

    x, src, dst, edges = (np.asarray(a) for a in (x, src, dst, edge_attr_32))
    N, D = x.shape
    E, FE = edges.shape
    n_pad = up(N, P) * P
    groups = up(up(E, GROUP), SLOTS) * SLOTS
    e_pad = groups * GROUP

    x_pad = np.zeros((n_pad, D), x.dtype)
    x_pad[:N] = x
    src_pad = np.zeros(e_pad, src.dtype)
    src_pad[:E] = src
    dst_pad = np.full(e_pad, PAD_DST, dst.dtype)
    dst_pad[:E] = dst
    ea_pad = np.zeros((e_pad, FE), edges.dtype)
    ea_pad[:E] = edges
    ea_t = np.ascontiguousarray(ea_pad.reshape(groups, TILES, P, FE).transpose(1, 3, 0, 2).reshape(TILES * FE, groups * P))
    arrays = {
        "x_nat": x_pad, "x_t": np.ascontiguousarray(x_pad.T),
        "src_cols": np.ascontiguousarray(src_pad.reshape(-1, P).T),
        "dst_rows": dst_pad.reshape(-1, SLOTS * GROUP),
        "dst_cols": np.ascontiguousarray(dst_pad.reshape(-1, P).T),
        "ea_t": ea_t,
        "W1n": L0_gnn_W1n, "b1n": L0_gnn_b1n, "W2n": L0_gnn_W2n, "b2n": L0_gnn_b2n,
        "W1e": L0_gnn_W1e, "b1e": L0_gnn_b1e, "W2e": L0_gnn_W2e, "b2e": L0_gnn_b2e,
        "res_w": L0_gnn_res_w, "dp_scale": L0_gnn_dp_scale, "gamma": L0_gnn_gamma, "beta": L0_gnn_beta,
        "W1_t": np.ascontiguousarray(np.asarray(L1_gnn_W).T), "b1": L1_gnn_b,
    }
    arrays = {k: np.ascontiguousarray(v) for k, v in arrays.items()}
    nc = bacc.Bacc("TRN2", target_bir_lowering=False, num_devices=1)
    args = [nc.dram_tensor(k, a.shape, _mybir.dt.from_np(a.dtype), kind="ExternalInput").ap() for k, a in arrays.items()]
    args.append(nc.dram_tensor("out", (N, D), F32, kind="ExternalOutput").ap())
    gnn_kernel(nc, E, *args)
    r = run_bass_kernel_spmd(nc, [arrays], core_ids=[0])
    return r.results[0]["out"]
```
